# Optimizing a Trainium2 kernel written in Bass

```python
import numpy as np
import jax
import jax.numpy as jnp

def _softmax(x, axis=-1):
    return jax.nn.softmax(x, axis=axis)
def _gelu(x):
    return jax.nn.gelu(x, approximate=True)
def _silu(x):
    return jax.nn.silu(x)
def _sigmoid(x):
    return jax.nn.sigmoid(x)
def _layernorm(x, axis=-1, eps=1e-5):
    m = jnp.mean(x, axis=axis, keepdims=True)
    v = jnp.var(x, axis=axis, keepdims=True)
    return (x - m) / jnp.sqrt(v + eps)
def _scatter_add(tgt, idx, src, axis=0):
    return tgt.at[idx].add(src)
def _segment_sum(src, seg, n):
    return jax.ops.segment_sum(src, seg, n)

kernel_name = 'mk_conv_preact_d1_conv_nchw32_8ab69b'

def setup_inputs(seed: int = 0):
    np.random.seed(seed)
    _w = jnp.asarray
    def _rec_inputs():
        import jax
        import jax.numpy as jnp
        _gk = jax.random.key(seed)
        x = -7.109e-05 + 0.9999 * jax.random.normal(jax.random.fold_in(_gk, 1), (8, 32, 512, 512), jnp.float32)
        return x
    x = _rec_inputs()
    def _L0_conv_setup():
        import jax, jax.numpy as jnp
        import numpy as np
        EPS = 1e-05

        def conv2d(x, w, b, padding=0, groups=1):
            out = jax.lax.conv_general_dilated(x, w, window_strides=(1, 1), padding=[(padding, padding), (padding, padding)], feature_group_count=groups, dimension_numbers=('NCHW', 'OIHW', 'NCHW'))
            return out + b[None, :, None, None]

        def avg_pool_3s2p1(x):
            s = jax.lax.reduce_window(x, 0.0, jax.lax.add, (1, 1, 3, 3), (1, 1, 2, 2), [(0, 0), (0, 0), (1, 1), (1, 1)])
            return s / 9.0

        def max_pool_2s2(x):
            return jax.lax.reduce_window(x, -jnp.inf, jax.lax.max, (1, 1, 2, 2), (1, 1, 2, 2), [(0, 0), (0, 0), (0, 0), (0, 0)])

        def channel_shuffle(x, groups=2):
            B, C, H, W = x.shape
            x = x.reshape(B, groups, C // groups, H, W)
            x = jnp.transpose(x, (0, 2, 1, 3, 4))
            return x.reshape(B, C, H, W)

        def batch_norm(x, gamma, beta):
            mean = jnp.mean(x, axis=(0, 2, 3), keepdims=True)
            var = jnp.var(x, axis=(0, 2, 3), keepdims=True)
            return (x - mean) * jax.lax.rsqrt(var + EPS) * gamma[None, :, None, None] + beta[None, :, None, None]
        key = jax.random.key(seed)
        dim, heads = (32, 4)
        B, H, W = (8, 512, 512)
        ks = jax.random.split(key, 16)
        sc = 0.05
        inp = {'x': jax.random.normal(ks[0], (B, dim, H, W), jnp.float32), 'qkvl_w': jax.random.normal(ks[1], (dim // 4 * heads, dim // 2, 1, 1), jnp.float32) * sc, 'qkvl_b': jax.random.normal(ks[2], (dim // 4 * heads,), jnp.float32) * sc, 'conv3x3_w': jax.random.normal(ks[3], (dim, dim // 4 * heads, 3, 3), jnp.float32) * sc, 'conv3x3_b': jax.random.normal(ks[4], (dim,), jnp.float32) * sc, 'conv1x1_w': jax.random.normal(ks[5], (dim // 2, dim, 1, 1), jnp.float32) * sc, 'conv1x1_b': jax.random.normal(ks[6], (dim // 2,), jnp.float32) * sc, 'conv1x1_2_w': jax.random.normal(ks[7], (dim // 2, dim // 4, 1, 1), jnp.float32) * sc, 'conv1x1_2_b': jax.random.normal(ks[8], (dim // 2,), jnp.float32) * sc, 'conv1x1_3_w': jax.random.normal(ks[9], (dim, dim // 2, 1, 1), jnp.float32) * sc, 'conv1x1_3_b': jax.random.normal(ks[10], (dim,), jnp.float32) * sc, 'dwc3x3_w': jax.random.normal(ks[11], (dim, 1, 3, 3), jnp.float32) * sc, 'dwc3x3_b': jax.random.normal(ks[12], (dim,), jnp.float32) * sc, 'bn_gamma': jnp.ones((dim,), jnp.float32), 'bn_beta': jnp.zeros((dim,), jnp.float32)}
        return inp
    _L0_conv_all = _L0_conv_setup()
    _L0_conv_in = {k: v for k, v in _L0_conv_all.items() if k in ('qkvl_w', 'qkvl_b', 'conv3x3_w', 'conv3x3_b', 'conv1x1_w', 'conv1x1_b', 'conv1x1_2_w', 'conv1x1_2_b', 'conv1x1_3_w', 'conv1x1_3_b', 'dwc3x3_w', 'dwc3x3_b', 'bn_gamma', 'bn_beta', )}
    del _L0_conv_all

    return {
        "x": x,
        "L0_conv_qkvl_w": _L0_conv_in["qkvl_w"],
        "L0_conv_qkvl_b": _L0_conv_in["qkvl_b"],
        "L0_conv_conv3x3_w": _L0_conv_in["conv3x3_w"],
        "L0_conv_conv3x3_b": _L0_conv_in["conv3x3_b"],
        "L0_conv_conv1x1_w": _L0_conv_in["conv1x1_w"],
        "L0_conv_conv1x1_b": _L0_conv_in["conv1x1_b"],
        "L0_conv_conv1x1_2_w": _L0_conv_in["conv1x1_2_w"],
        "L0_conv_conv1x1_2_b": _L0_conv_in["conv1x1_2_b"],
        "L0_conv_conv1x1_3_w": _L0_conv_in["conv1x1_3_w"],
        "L0_conv_conv1x1_3_b": _L0_conv_in["conv1x1_3_b"],
        "L0_conv_dwc3x3_w": _L0_conv_in["dwc3x3_w"],
        "L0_conv_dwc3x3_b": _L0_conv_in["dwc3x3_b"],
        "L0_conv_bn_gamma": _L0_conv_in["bn_gamma"],
        "L0_conv_bn_beta": _L0_conv_in["bn_beta"],
    }

def reference(x, L0_conv_qkvl_w, L0_conv_qkvl_b, L0_conv_conv3x3_w, L0_conv_conv3x3_b, L0_conv_conv1x1_w, L0_conv_conv1x1_b, L0_conv_conv1x1_2_w, L0_conv_conv1x1_2_b, L0_conv_conv1x1_3_w, L0_conv_conv1x1_3_b, L0_conv_dwc3x3_w, L0_conv_dwc3x3_b, L0_conv_bn_gamma, L0_conv_bn_beta):
    import jax
    import jax.numpy as jnp
    def _L0_conv_ref(x, qkvl_w, qkvl_b, conv3x3_w, conv3x3_b, conv1x1_w, conv1x1_b, conv1x1_2_w, conv1x1_2_b, conv1x1_3_w, conv1x1_3_b, dwc3x3_w, dwc3x3_b, bn_gamma, bn_beta):
        import jax, jax.numpy as jnp
        import numpy as np
        EPS = 1e-05

        def conv2d(x, w, b, padding=0, groups=1):
            out = jax.lax.conv_general_dilated(x, w, window_strides=(1, 1), padding=[(padding, padding), (padding, padding)], feature_group_count=groups, dimension_numbers=('NCHW', 'OIHW', 'NCHW'))
            return out + b[None, :, None, None]

        def avg_pool_3s2p1(x):
            s = jax.lax.reduce_window(x, 0.0, jax.lax.add, (1, 1, 3, 3), (1, 1, 2, 2), [(0, 0), (0, 0), (1, 1), (1, 1)])
            return s / 9.0

        def max_pool_2s2(x):
            return jax.lax.reduce_window(x, -jnp.inf, jax.lax.max, (1, 1, 2, 2), (1, 1, 2, 2), [(0, 0), (0, 0), (0, 0), (0, 0)])

        def channel_shuffle(x, groups=2):
            B, C, H, W = x.shape
            x = x.reshape(B, groups, C // groups, H, W)
            x = jnp.transpose(x, (0, 2, 1, 3, 4))
            return x.reshape(B, C, H, W)

        def batch_norm(x, gamma, beta):
            mean = jnp.mean(x, axis=(0, 2, 3), keepdims=True)
            var = jnp.var(x, axis=(0, 2, 3), keepdims=True)
            return (x - mean) * jax.lax.rsqrt(var + EPS) * gamma[None, :, None, None] + beta[None, :, None, None]
        heads = 4
        B, C, H, W = x.shape
        gelu = lambda t: jax.nn.gelu(t, approximate=False)
        x1, x2 = (x[:, :C // 2], x[:, C // 2:])
        x2 = gelu(conv2d(x2, qkvl_w, qkvl_b))
        x2 = jax.nn.relu(conv2d(x2, conv3x3_w, conv3x3_b, padding=1))
        x2 = conv2d(x2, conv1x1_w, conv1x1_b)
        x1h = gelu(conv2d(x1, qkvl_w, qkvl_b)).reshape(B, heads, C // heads, H, W)
        q = jnp.sum(x1h[:, :-3], axis=1)
        k = x1h[:, -3]
        v = x1h[:, -2].reshape(B, C // 4, H * W)
        qf = avg_pool_3s2p1(q).reshape(B, C // 4, -1)
        kf = max_pool_2s2(k).reshape(B, C // 4, -1)
        scores = jnp.einsum('bqn,bkn->bqk', qf, kf)
        qk = jnp.transpose(jax.nn.softmax(scores, axis=1), (0, 2, 1))
        x1a = jnp.einsum('bij,bjn->bin', qk, v).reshape(B, C // 4, H, W)
        x1a = conv2d(x1a, conv1x1_2_w, conv1x1_2_b)
        xc = jnp.concatenate([x1a, x2], axis=1)
        xc = channel_shuffle(xc, groups=2)
        xc = gelu(batch_norm(conv2d(xc, dwc3x3_w, dwc3x3_b, padding=1, groups=C), bn_gamma, bn_beta))
        x1o = conv2d(x1a, conv1x1_3_w, conv1x1_3_b)
        return xc + x1o

    def _gn(v, G=16, eps=1e-5):
        B_, C_, H_, W_ = v.shape
        g = v.reshape(B_, G, C_ // G, H_, W_)
        m = jnp.mean(g, axis=(2, 3, 4), keepdims=True)
        s = jnp.var(g, axis=(2, 3, 4), keepdims=True)
        return ((g - m) / jnp.sqrt(s + eps)).reshape(v.shape)

    def _ln_c(v, eps=1e-6):
        m = jnp.mean(v, axis=1, keepdims=True)
        s = jnp.var(v, axis=1, keepdims=True)
        return (v - m) / jnp.sqrt(s + eps)

    def _ln_t(v, eps=1e-5):
        m = jnp.mean(v, axis=-1, keepdims=True)
        s = jnp.var(v, axis=-1, keepdims=True)
        return (v - m) / jnp.sqrt(s + eps)

    def _to_tokens(v):
        B_, C_, H_, W_ = v.shape
        return v.reshape(B_, C_, H_ * W_).transpose(0, 2, 1)
    def _from_tokens(t, like):
        B_, C_, H_, W_ = like.shape
        return t.transpose(0, 2, 1).reshape(B_, C_, H_, W_)

    x = x + _L0_conv_ref(_gn(x), L0_conv_qkvl_w, L0_conv_qkvl_b, L0_conv_conv3x3_w, L0_conv_conv3x3_b, L0_conv_conv1x1_w, L0_conv_conv1x1_b, L0_conv_conv1x1_2_w, L0_conv_conv1x1_2_b, L0_conv_conv1x1_3_w, L0_conv_conv1x1_3_b, L0_conv_dwc3x3_w, L0_conv_dwc3x3_b, L0_conv_bn_gamma, L0_conv_bn_beta)
    return x


_drawn_inputs = setup_inputs


def setup_inputs(seed=0):
    import zlib

    import numpy as np

    out = dict(_drawn_inputs(seed))
    spreads = {'L0_conv_bn_gamma': (1.0, 0.2), 'L0_conv_bn_beta': (0.0, 0.1)}
    factors = {'L0_conv_conv1x1_3_w': 5.878}
    for name, (base, spread) in spreads.items():
        noise = np.random.default_rng([zlib.crc32(name.encode()), seed]).standard_normal(out[name].shape)
        drawn = base * np.exp(spread * noise) if base else spread * noise
        out[name] = jnp.asarray(drawn.astype(out[name].dtype))
    for name, factor in factors.items():
        out[name] = (out[name] * factor).astype(out[name].dtype)
    return out
```

```python
from contextlib import ExitStack

import concourse.bass as bass
from concourse import mybir
from concourse.alu_op_type import AluOpType as ALU

F32 = mybir.dt.float32
ACT = mybir.ActivationFunctionType
AX_X = mybir.AxisListType.X

C = 32
W = 512
XR = 4
TR = 16
GN_EPS = BN_EPS = 1e-5


def preact_kernel(nc, x, w_qkv, b_qkv, w_c3, b_c3, w_c1, b_c1, bn_dw, w_dw2, w_dw1, dw_sum, b_2rep, b_dw,
                  w2t, w3t, w3rep, b3rep, row_mask, gn_mix, bn_mix, ident, pool_sum, score_mask, score_fold,
                  keep_first, out, v_dram, d_dram):
    B, H = x.shape[0], x.shape[1]
    NT = H // TR
    K = H // XR
    NZ = H // 8
    VR = v_dram.shape[1]
    assert NT % 2 == 0 and NT >= 6
    xrows = x.rearrange("b h c w -> (b h c) w")
    vrows = v_dram.rearrange("b h c w -> (b h c) w")
    drows = d_dram.rearrange("b h c w -> (b h c) w")
    xpair = x.rearrange("b h (i e) w -> (b h i) (e w)", e=2)
    opair = out.rearrange("b h (i e) w -> (b h i) (e w)", e=2)

    with ExitStack() as ctx:
        def sb(name, shape):
            return ctx.enter_context(nc.sbuf_tensor("s_" + name, shape, F32))

        def sem(name):
            return ctx.enter_context(nc.semaphore(name))

        wqkv = sb("wqkv", [128, 4, 128]);   bqkv = sb("bqkv", [128, 4])
        wc3 = sb("wc3", [128, 9, 64]);      bc3 = sb("bc3", [128, 2])
        wc1 = sb("wc1", [128, 2, 64]);      bc1 = sb("bc1", [128, 2])
        bndw = sb("bndw", [128, 2, 2]);     wd2 = sb("wd2", [128, 9, 64])
        td1 = sb("td1", [128, 24, 2, 16]);  dws = sb("dws", [128, 3, 3, 3])
        b2r = sb("b2r", [128, 1]);          bdw = sb("bdw", [128, 2])
        w2T = sb("w2T", [8, 16]);           w3T = sb("w3T", [16, 32])
        w3r = sb("w3r", [16, 2, 128]);      b3r = sb("b3r", [128, 2])
        b2c = sb("b2c", [16, 1])
        rmask = sb("rmask", [128, 8, 2]);   gmix = sb("gmix", [128, 128])
        bmix = sb("bmix", [128, 128]);      idn = sb("idn", [128, 128])
        psumw = sb("psumw", [128, 2, 64]);  smask = sb("smask", [64, 64])
        sfold = sb("sfold", [64, 128]);       keep0 = sb("keep0", [128, 1])
        ws = sb("ws", [128, 4, 128]);       bs = sb("bs", [128, 4])
        mv = sb("mv", [128, 2]);            mg = sb("mg", [128, 1])
        dev = sb("dev", [128, 1]);          dv2 = sb("dv2", [128, 1]);  rs = sb("rs", [128, 1]);  vs = sb("vs", [128, 1]);  sq = sb("sq", [128, 1]);  nt = sb("nt", [128, 1])
        scm = sb("scm", [64, 64]);          sc8 = sb("sc8", [8, 8]);    scd = sb("scd", [8, 8])
        smx = sb("smx", [8, 1]);            sce = sb("sce", [8, 8]);    ssum = sb("ssum", [8, 1])
        sinv = sb("sinv", [8, 1]);          attn = sb("attn", [8, 16, 8])
        mo = sb("mo", [16, 128])
        mfac = sb("mfac", [128, B, 48])
        d1w = sb("d1w", [128, 24, 2, 16])
        x1w = sb("x1w", [128, 2, 8, 2, 16])
        d1c = sb("d1c", [128, 3]);          d1x = sb("d1x", [128, 3, 2])
        dwr = sb("dwr", [128, 3, 3])
        x1c = sb("x1c", [128, 2])
        ab = sb("ab", [128, 2, 2]);         bt = sb("bt", [128, 3]); mvb = sb("mvb", [128, 2, 2])
        mgb = sb("mgb", [128, 2]); devb = sb("devb", [128, 2]); dvb2 = sb("dvb2", [128, 2]); rsb = sb("rsb", [128, 2]); vsb = sb("vsb", [128, 2]); sqb = sb("sqb", [128, 2]); ntb = sb("ntb", [128, 2])
        tmpb = sb("tmpb", [128, 2]);  tmb2 = sb("tmb2", [128, 2])
        gst = sb("gst", [128, K, 6]);       dst1 = sb("dst1", [128, B * NZ, 6])
        dst2 = sb("dst2", [128, B * NZ, 6])
        xb = sb("xb", [128, 2, 4, W])
        xs = sb("xs", [128, 2, 4, W])
        gb = sb("gb", [128, 8, W + 2])
        rb = sb("rb", [128, 2, W])
        zb = sb("zb", [128, 4, W + 2])
        db = sb("db", [128, 2, W])
        qb = sb("qb", [128, W + 2]);        kb = sb("kb", [128, W])
        vb = sb("vb", [128, 2, W])
        qh = sb("qh", [128, W // 2]);       hq = sb("hq", [128, 2, W // 2]);  hk = sb("hk", [128, W // 2])
        qT = sb("qT", [128, 2, 64]);        kT = sb("kT", [128, 2, 64])
        va = sb("va", [128, 2, 2, W + 2])
        yb = sb("yb", [128, 2, 2, 2, W])
        dl = sb("dl", [128, 2, 2, W])
        ps = ctx.enter_context(nc.psum_tensor("ps", [128, 8, W], F32))

        s_cst = sem("consts_loaded")
        s_x = [sem("x_loaded_even"), sem("x_loaded_odd")]
        s_xs = [sem("xs_loaded_even"), sem("xs_loaded_odd")]
        s_va = [sem("va_loaded_even"), sem("va_loaded_odd")]
        s_dl = [sem("d_loaded_even"), sem("d_loaded_odd")]
        s_vst = [sem("v_stored_even"), sem("v_stored_odd")]
        s_dst = [sem("d_stored_even"), sem("d_stored_odd")]
        s_ost = [sem("out_stored_even"), sem("out_stored_odd")]
        s_zv = sem("v_borders_stored")
        s_pad = sem("pads_zeroed")
        s_g7 = sem("above_image_zeroed")
        s_q2 = sem("block_product_done"); s_g = sem("g_written"); s_cv = sem("conv_done")
        s_r = sem("relu_written"); s_z1 = sem("conv1x1_done"); s_z = sem("z_written")
        s_q = sem("qkv_product_done"); s_qa = sem("qkv_written")
        s_h = sem("pool_rows_done"); s_hs = sem("pool_partial_done")
        s_tp = sem("pooled_transposed"); s_te = sem("pooled_copied"); s_sc = sem("scores_added")
        s_d = sem("dw_done"); s_de = sem("dw_written"); s_dn = sem("dw_stats_done")
        s_gs = sem("x_stats_done")
        s_f = sem("dve_chain"); s_k = sem("d1_constants"); s_pw = sem("rstd_steps"); s_sq = sem("root_written"); s_zz = sem("below_image_zeroed"); s_m = sem("small_product_done"); s_ws = sem("weights_scaled")
        s_bs = sem("bias_ready"); s_ex = sem("exp_done"); s_dw = sem("dw1_weights_ready")
        s_a1 = sem("dw1_done"); s_a1c = sem("dw1_columns_fixed"); s_a1e = sem("dw1_written")
        s_a1n = sem("dw1_stats_done")
        s_fa = sem("last_dw1_done"); s_fc = sem("last_columns_fixed"); s_fx = sem("last_x1o_done")
        s_fg = sem("last_gelu_done"); s_ft = sem("last_residual_done"); s_fo = sem("last_sum_done")
        s_bn = sem("bn_ready"); s_fw = sem("last_weights_ready")

        small = [(w_qkv, wqkv), (b_qkv, bqkv), (w_c3, wc3), (b_c3, bc3), (w_c1, wc1), (b_c1, bc1), (bn_dw, bndw),
                 (w_dw2, wd2), (w_dw1, td1), (dw_sum, dws), (b_2rep, b2r), (b_dw, bdw), (w2t, w2T), (w3t, w3T),
                 (w3rep, w3r), (b3rep, b3r), (row_mask, rmask), (gn_mix, gmix), (bn_mix, bmix), (ident, idn),
                 (pool_sum, psumw), (score_mask, smask), (score_fold, sfold), (keep_first, keep0)]
        NCONST = 16 * (len(small) + 1)

        block = ctx.enter_context(nc.Block())

        def batches(eng, body):
            body(0, True)
            with eng.Fori(1, B - 1) as b:
                body(b, True)
            body(B - 1, False)

        def steps(eng, body):
            body(0, 0, 0, True, False)
            body(1, 0, 1, False, False)
            with eng.Fori(1, NT // 2 - 1) as i:
                body(i * 2, i, 0, False, False)
                body(i * 2 + 1, i, 1, False, False)
            body(NT - 2, NT // 2 - 1, 0, False, False)
            body(NT - 1, NT // 2 - 1, 1, False, True)

        def static(v, below=1):
            return isinstance(v, int) and v < below

        NP = NT // 2
        CV = 2 * NT + 1
        NRL = 4 * NT + 1
        NZB = 2 * NT + 1
        SM = 7
        GCH, ACH = 6, 11

        def at(b, i):
            return 16 * (b * NP + i) + 16

        @block.sync
        def _(sp):
            for src, dst in small:
                sp.dma_start(dst[:], src).then_inc(s_cst, 16)
            sp.dma_start(b2c[:], b_2rep[0:16, :]).then_inc(s_cst, 16)
            sp.wait_ge(s_pad, 4)
            for b in range(B):
                sp.dma_start(vrows[b * VR * 8:b * VR * 8 + 8, :], va[0:8, 0, 0, 0:W]).then_inc(s_zv, 16)
                sp.dma_start(vrows[(b * VR + H + 1) * 8:(b + 1) * VR * 8, :], va[0:8, 0, 0, 0:W]).then_inc(s_zv, 16)

            def load_x(b, T, p):
                sp.dma_start(xb[:, p], xrows[bass.ds((b * H + T * TR) * C, TR * C), :]
                             .rearrange("(k p) w -> p k w", p=128)).then_inc(s_x[p], 16)

            def load_stats(b, T, p):
                sp.dma_start(xs[:, p], xrows[bass.ds((b * H + T * TR) * C, TR * C), :]
                             .rearrange("(k p) w -> p k w", p=128)).then_inc(s_xs[p], 16)

            def first_stats(T, i, p, first, last):
                if not static(T, 2):
                    sp.wait_ge(s_gs, 4 * (T - 1))
                load_stats(0, T, p)
            steps(sp, first_stats)

            def batch(b, nxt):
                def main(T, i, p, first, last):
                    n = b * NT + T
                    if nxt:
                        sp.wait_ge(s_gs, 4 * ((b + 1) * NT + T - 1))
                        load_stats(b + 1, T, p)
                    sp.wait_ge(s_qa, 3 * (n + 1))
                    sp.dma_start(vrows[bass.ds((b * VR + 1 + T * TR) * 8, 128), :], vb[:, p]).then_inc(s_vst[p], 16)
                    if not (isinstance(T, int) and T >= NT - 2):
                        sp.wait_ge(s_q, 3 * (n + 1))
                        load_x(b, T + 2, p)
                    if not first:
                        for q in range(2):
                            store_d(b, 2 * T - 2 + q, q)
                    if last:
                        for q in range(2):
                            store_d(b, 2 * NT - 2 + q, q)

                def store_d(b, t, q):
                    sp.wait_ge(s_de, b * NZ + t + 1)
                    if q == 0:
                        sp.dma_start(drows[bass.ds((b * H + t * 8) * 16, 128), :], db[:, q]).then_inc(s_dst[q], 16)
                    else:
                        sp.dma_start(drows[bass.ds((b * H + t * 8) * 16, 64), :], db[64:128, q]).then_inc(s_dst[q], 16)
                        sp.dma_start(drows[bass.ds((b * H + t * 8 + 4) * 16, 64), :], db[0:64, q]).then_inc(s_dst[q], 16)
                steps(sp, main)

                if nxt:
                    sp.wait_ge(s_q, 3 * (b + 1) * NT)
                    for q in range(2):
                        load_x(b + 1, q, q)
                for q in range(2):
                    sp.wait_ge(s_vst[q], at(b, NP - 1))

                def dw1(T, i, p, first, last):
                    sp.wait_ge(s_a1, 2 * b * NT if static(T, 2) else 2 * (b * NT + T) - 2)
                    load_va(b, T, p)
                steps(sp, dw1)

            def load_va(b, T, p):
                sp.dma_start(va[:, p, 0, 1:W + 1], vrows[bass.ds((b * VR + T * TR) * 8, 128), :]).then_inc(s_va[p], 16)
                sp.dma_start(va[:, p, 1, 1:W + 1], vrows[bass.ds((b * VR + T * TR + 2) * 8, 128), :]).then_inc(s_va[p], 16)

            sp.wait_ge(s_zv, 32 * B)
            for q in range(2):
                load_x(0, q, q)
            batches(sp, batch)
            sp.wait_ge(s_a1, 2 * NT * B)
            sp.wait_ge(s_q, 3 * B * NT)
            sp.wait_ge(s_dst[0], B * NT * 16)
            sp.wait_ge(s_dst[1], B * NT * 32)

            def last_batch(b):
                def last_pass(T, i, p, first, last):
                    n = b * NT + T
                    m = b * NP + i
                    if not (static(b) and static(T, 2)):
                        sp.wait_ge(s_ost[p], m * 32)
                    load_va(b, T, p)
                    sp.dma_start(dl[:, p], drows[bass.ds((b * H + T * TR) * 16, 256), :]
                                 .rearrange("(h p) w -> p h w", p=128)).then_inc(s_dl[p], 16)
                    sp.dma_start(xb[:, p].rearrange("p (h e) w -> p h (e w)", h=2),
                                 xpair[bass.ds((b * H + T * TR) * 16, 256), :]
                                 .rearrange("(h p) w -> p h w", p=128)).then_inc(s_x[p], 16)
                steps(sp, last_pass)
            last_batch(0)
            with sp.Fori(1, B) as b:
                last_batch(b)

        @block.gpsimd
        def _(pool):
            pool.memset(gb[:], 0.0).then_inc(s_pad, 1)
            pool.memset(zb[:], 0.0).then_inc(s_pad, 1)
            pool.memset(va[:], 0.0).then_inc(s_pad, 1)
            pool.memset(qb[:], 0.0).then_inc(s_pad, 1)

            def last_batch(b):
                def last_pass(T, i, p, first, last):
                    n = b * NT + T
                    for h in range(2):
                        pool.wait_ge(s_fo, 2 * n + h + 1)
                        pool.dma_start(opair[bass.ds((b * H + T * TR + 8 * h) * 16, 128), :],
                                       xb[:, p, 2 * h:2 * h + 2].rearrange("p e w -> p (e w)")).then_inc(s_ost[p], 16)
                steps(pool, last_pass)
            last_batch(0)
            with pool.Fori(1, B) as b:
                last_batch(b)
            for p in range(2):
                pool.wait_ge(s_ost[p], B * NP * 32)

        @block.tensor
        def _(pe):
            mm = nc.tensor.matmul
            pe.wait_ge(s_cst, NCONST)
            pe.wait_ge(s_pad, 4)

            def batch(b, nxt):
                pe.wait_ge(s_a1e, 2 * NT * b)
                pe.wait_ge(s_f, b * (GCH + ACH) + 1)
                mm(ps[:, 4, 0:1], gmix[:], mv[:, 0:1], start=True, stop=True).then_inc(s_m, 1)
                pe.wait_ge(s_f, b * (GCH + ACH) + 5)
                mm(ps[:, 4, 1:2], gmix[:], dv2[:], start=True, stop=True).then_inc(s_m, 1)
                pe.wait_ge(s_ws, b + 1)
                for g in range(4):
                    last = mm(ps[:, 4, 2 + g:3 + g], ws[:, g, :], mg[:], start=True, stop=True)
                last.then_inc(s_m, 1)

                def product(k, p, j):
                    if not static(k, 2):
                        pe.wait_ge(s_g, b * K + k - 1)
                    mm(ps[:, j % 2, :], ws[:, 0, :], xb[:, p, j], start=True, stop=True).then_inc(s_q2, 1)

                def qkv(n, part, p, bank):
                    for j in range(4):
                        last = mm(ps[32 * j:32 * j + 32, bank, :], ws[:, 1 + part, 0:32], xb[:, p, j], start=True, stop=True)
                    return last

                def conv(lists):
                    last = None
                    for step in range(max(len(l) for l in lists)):
                        for l in lists:
                            if step < len(l):
                                o, w, m, st, sp_ = l[step]
                                last = mm(o, w, m, start=st, stop=sp_)
                    return last

                def taps(o, terms):
                    return [(o, w, m, i == 0, i == len(terms) - 1) for i, (w, m) in enumerate(terms)]

                def conv3x3(p, J):
                    s0 = (4 * p + 2 * J) % 8
                    def across(s):
                        above = [(wc3[:, 3 + d, :], gb[:, (s - 1) % 8, d:d + W]) for d in range(3)]
                        here = [(wc3[:, 6 + d, :], gb[:, s, d:d + W]) for d in range(3)]
                        return above + here
                    def inside(s):
                        return [(wc3[:, d, :], gb[:, s, d:d + W]) for d in range(3)]
                    left = taps(ps[0:64, 2, :], across(s0)) + taps(ps[0:64, 3, :], inside(s0 + 1))
                    right = taps(ps[64:128, 2, :], inside(s0)) + taps(ps[64:128, 3, :], across(s0 + 1))
                    return conv([left, right])

                def conv1x1():
                    mm(ps[0:64, 4, :], wc1[:, 0, :], rb[:, 0], start=True, stop=True)
                    mm(ps[64:128, 4, :], wc1[:, 1, :], rb[:, 1], start=True, stop=True).then_inc(s_z1, 1)

                def dw2(s0):
                    def low(s):
                        return [(wd2[:, d, :], zb[:, s % 4, d:d + W]) for d in range(3)]
                    def high(s):
                        return ([(wd2[:, 3 + d, :], zb[:, s % 4, d:d + W]) for d in range(3)] +
                                [(wd2[:, 6 + d, :], zb[:, (s + 1) % 4, d:d + W]) for d in range(3)])
                    left = taps(ps[0:64, 5, :], low(s0)) + taps(ps[0:64, 6, :], high(s0 + 1))
                    right = taps(ps[64:128, 5, :], high(s0)) + taps(ps[64:128, 6, :], low(s0 + 1))
                    return conv([left, right])

                def dw2_pair(t, s0):
                    pe.wait_ge(s_z, b * NZB + t + 3)
                    dw2(s0).then_inc(s_d, 2)

                pe.wait_ge(s_bs, b + 1)
                pe.wait_ge(s_x[0], at(b, 0))
                pe.wait_ge(s_g, b * K)
                product(0, 0, 0)
                product(1, 0, 1)
                pe.wait_ge(s_g7, b + 1)

                def main(T, i, p, first, last):
                    n = b * NT + T
                    product(4 * T + 2, p, 2)
                    product(4 * T + 3, p, 3)
                    if not first:
                        pe.wait_ge(s_r, b * NRL + 4 * T)
                        pe.wait_ge(s_z, b * NZB + 2 * T - 1)
                        conv1x1()
                    if first:
                        pe.wait_ge(s_de, b * NZ)
                    else:
                        if not static(T, 2):
                            pe.wait_ge(s_de, b * NZ + 2 * T - 2)
                    qkv(n, 0, p, 5).then_inc(s_q, 1)
                    qkv(n, 1, p, 6).then_inc(s_q, 1)
                    pe.wait_ge(s_g, b * K + 4 * T + 2)
                    conv3x3(p, 0).then_inc(s_cv, 1)
                    pe.wait_ge(s_qa, 3 * n + 1)
                    v = qkv(n, 2, p, 5)
                    v.then_inc(s_q, 1)
                    if not last:
                        pe.wait_ge(s_x[1 - p], at(b, i + p))
                        product(4 * T + 4, 1 - p, 0)
                        product(4 * T + 5, 1 - p, 1)
                    pe.wait_ge(s_r, b * NRL + 4 * T + 2)
                    if not first:
                        pe.wait_ge(s_z, b * NZB + 2 * T)
                    conv1x1()
                    pe.wait_ge(s_h, 3 * (n + 1))
                    pe.wait_ge(s_qa, 3 * n + 2)
                    for h in range(2):
                        cols = slice(128 * h, 128 * h + 128)
                        mm(ps[:, 6, 64 * h:64 * h + 64], hq[:, p, cols], psumw[:, 0, :], start=(h == 0), stop=first,
                           skip_group_check=True)
                        if not first:
                            mm(ps[:, 6, 64 * h:64 * h + 64], hq[:, 1 - p, cols], psumw[:, 1, :], start=False, stop=True,
                               skip_group_check=True)
                    for h in range(2):
                        cols = slice(128 * h, 128 * h + 128)
                        tk = mm(ps[:, 6, 128 + 128 * h:256 + 128 * h], hk[:, cols], idn[:], start=False, stop=True,
                                skip_group_check=True)
                    tk.then_inc(s_tp, 1)
                    pe.wait_ge(s_g, b * K + 4 * T + 4)
                    conv3x3(p, 1).then_inc(s_cv, 1)
                    pe.wait_ge(s_qa, 3 * n + 3)
                    pe.wait_ge(s_te, 2 * n + 2)
                    if not first:
                        dw2_pair(2 * T - 2, (2 * p - 2) % 4)
                    for h in range(2):
                        sc = mm(ps[0:64, 7, 0:64], kT[:, h, :], qT[:, h, :], start=(first and h == 0),
                                stop=(last and h == 1), skip_group_check=True)
                    sc.then_inc(s_sc, 1)
                steps(pe, main)

                pe.wait_ge(s_r, b * NRL + 4 * NT)
                pe.wait_ge(s_z, b * NZB + 2 * NT - 1)
                conv1x1()
                conv([taps(ps[0:64, 2, :], [(wc3[:, 3 + d, :], gb[:, 7, d:d + W]) for d in range(3)])]).then_inc(s_cv, 1)
                pe.wait_ge(s_r, b * NRL + 4 * NT + 1)
                pe.wait_ge(s_z, b * NZB + 2 * NT)
                mm(ps[0:64, 4, :], wc1[0:32, 0, :], rb[0:32, 0], start=True, stop=True).then_inc(s_z1, 1)
                pe.wait_ge(s_de, b * NZ + 2 * NT - 2)
                dw2_pair(2 * NT - 2, (2 * NT - 2) % 4)

                pe.wait_ge(s_f, b * (GCH + ACH) + GCH + 1)
                mm(ps[:, 4, 0:64], sfold[:], scm[:], start=True, stop=True).then_inc(s_m, 1)
                pe.wait_ge(s_f, b * (GCH + ACH) + GCH + 8)
                mm(ps[:, 4, 64:80], attn[:].rearrange("i l j -> i (l j)"), w2T[:], start=True, stop=True).then_inc(s_m, 1)
                mm(ps[0:16, 3, 0:128], w2T[:], attn[:].rearrange("i l j -> i (l j)"), start=True, stop=True).then_inc(s_m, 1)
                pe.wait_ge(s_f, b * (GCH + ACH) + GCH + 10)
                mm(ps[:, 4, 96:128], mo[:], w3T[:], start=True, stop=True).then_inc(s_m, 1)

                pe.wait_ge(s_dw, b + 1)

                def dw1(T, i, p, first, last):
                    n = b * NT + T
                    pe.wait_ge(s_va[p], 2 * at(b, i))
                    for h in range(2):
                        if not static(T, 2):
                            pe.wait_ge(s_a1e, 2 * n + h - 3)
                        dwconv1(mm, 2 * p + h, p, h).then_inc(s_a1, 1)
                steps(pe, dw1)

            def dwconv1(mm, bank, p, h):
                for d in range(3):
                    for m in range(4):
                        last = mm(ps[32 * m:32 * m + 32, bank, :],
                                  d1w[:, (4 * h + m) * 3 + d].rearrange("p r i -> p (r i)"), va[:, p, h, d:d + W],
                                  start=(d == 0), stop=(d == 2))
                return last

            batches(pe, batch)

            pe.wait_ge(s_a1e, 2 * NT * B)
            for e in range(2):
                last = mm(ps[:, 7, e:e + 1], w3r[:, e, :], b2c[:], start=True, stop=True)
            last.then_inc(s_m, 1)
            pe.wait_ge(s_f, B * (GCH + ACH) + 2)
            mm(ps[:, 7, 4:6], bmix[:], mvb[:, :, 0], start=True, stop=True).then_inc(s_m, 1)
            pe.wait_ge(s_f, B * (GCH + ACH) + 6)
            mm(ps[:, 7, 6:8], bmix[:], dvb2[:], start=True, stop=True).then_inc(s_m, 1)

            def last_batch(b):
                pe.wait_ge(s_fw, 3 * b + 3)

                def last_pass(T, i, p, first, last):
                    n = b * NT + T
                    pe.wait_ge(s_va[p], 2 * at(B + b, i))
                    for h in range(2):
                        if not (static(b) and static(T, 2)):
                            pe.wait_ge(s_fg, 4 * n + 2 * h - 6)
                        dwconv1(mm, 2 * p + h, p, h).then_inc(s_fa, 1)
                        if not (static(b) and first):
                            pe.wait_ge(s_ft, 2 * n + h - 1)
                        for e in range(2):
                            for m in range(4):
                                o = mm(ps[32 * m:32 * m + 32, 4 + 2 * h + e, :],
                                       x1w[:, e, 4 * h + m].rearrange("p r i -> p (r i)"), va[:, p, h, 1:1 + W],
                                       start=True, stop=True)
                            o.then_inc(s_fx, 1)
                steps(pe, last_pass)
            last_batch(0)
            with pe.Fori(1, B) as b:
                last_batch(b)

        @block.scalar
        def _(act):
            fn = nc.scalar.activation
            act.wait_ge(s_cst, NCONST)
            act.wait_ge(s_pad, 4)

            def batch(b, nxt):
                act.wait_ge(s_f, b * (GCH + ACH) + 6)
                fn(sq[:], vs[:], ACT.Sqrt).then_inc(s_sq, 1)
                act.wait_ge(s_bs, b + 1)

                def main(T, i, p, first, last):
                    n = b * NT + T

                    def gelu(j):
                        slot = (4 * p + j) % 8
                        act.wait_ge(s_q2, b * K + 4 * T + j + 1)
                        if static(T, 2) and 4 * T + j < 7:
                            act.wait_ge(s_cv, b * CV)
                        else:
                            act.wait_ge(s_cv, b * CV + 2 * T + (j - 5) // 2)
                        fn(gb[:, slot, 1:W + 1], ps[:, j % 2, :], ACT.Gelu, bias=bs[:, 0:1]).then_inc(s_g, 1)

                    def gelu_qkv(part, dst):
                        act.wait_ge(s_q, 3 * n + part + 1)
                        fn(dst, ps[:, 5 + part % 2, :], ACT.Gelu, bias=bs[:, 1 + part:2 + part]).then_inc(s_qa, 1)

                    if first:
                        gelu(0)
                        gelu(1)
                    gelu(2)
                    gelu(3)
                    act.wait_ge(s_h, 3 * n)
                    gelu_qkv(0, qb[:, 1:W + 1])
                    gelu_qkv(1, kb[:])
                    act.wait_ge(s_vst[p], 16 * (b * NP + i))
                    gelu_qkv(2, vb[:, p])
                    if not last:
                        gelu(4)
                        gelu(5)
                    if not first:
                        write_d(T - 1, static(T, 2))
                    if last:
                        write_d(NT - 1, False)

                def write_d(u, head):
                    act.wait_ge(s_d, b * NZ + 2 * u + 2)
                    for q in range(2):
                        act.wait_ge(s_dn, b * NZ if head else b * NZ + 2 * u + q - 1)
                        act.wait_ge(s_dst[q], (16 if q == 0 else 32) * (b * NT + u))
                        fn(db[:, q], ps[:, 5 + q, :], ACT.Identity, bias=bdw[:, 1:2]).then_inc(s_de, 1)

                steps(act, main)

                act.wait_ge(s_f, b * (GCH + ACH) + GCH + 4)
                fn(sce[:], scd[:], ACT.Exp).then_inc(s_ex, 1)

                def dw1(T, i, p, first, last):
                    n = b * NT + T
                    for h in range(2):
                        act.wait_ge(s_a1c, 2 * n + h + 1)
                        act.wait_ge(s_a1n, 2 * NT * b if static(T, 2) else 2 * n + h - 3)
                        v = 1 if first and h == 0 else 2 if last and h == 1 else 0
                        fn(yb[:, p, h, 0], ps[:, 2 * p + h, :], ACT.Identity, bias=d1c[:, v:v + 1]).then_inc(s_a1e, 1)
                steps(act, dw1)
            batches(act, batch)

            act.wait_ge(s_f, B * (GCH + ACH) + 7)
            fn(sqb[:], vsb[:], ACT.Sqrt).then_inc(s_sq, 1)
            act.wait_ge(s_bn, 1)

            def last_batch(b):
                def last_pass(T, i, p, first, last):
                    n = b * NT + T
                    act.wait_ge(s_dl[p], at(b, i))
                    for h in range(2):
                        act.wait_ge(s_fc, 2 * n + h + 1)
                        if not (static(b) and static(T, 2)):
                            act.wait_ge(s_fo, 2 * n + h - 3)
                        v = 1 if first and h == 0 else 2 if last and h == 1 else 0
                        fn(yb[:, p, h, 0], ps[:, 2 * p + h, :], ACT.Gelu, bias=bt[:, v:v + 1],
                           scale=ab[:, 0, 0:1]).then_inc(s_fg, 1)
                        fn(yb[:, p, h, 1], dl[:, p, h], ACT.Gelu, bias=ab[:, 1, 1:2],
                           scale=ab[:, 1, 0:1]).then_inc(s_fg, 1)
                steps(act, last_pass)
            last_batch(0)
            with act.Fori(1, B) as b:
                last_batch(b)

        @block.vector
        def _(dve):
            V = nc.vector
            dve.wait_ge(s_cst, NCONST)
            dve.wait_ge(s_pad, 4)

            V.tensor_reduce(dwr[:].rearrange("p v d -> p (v d)"), dws[:].rearrange("p v d y -> p (v d) y"), AX_X,
                            ALU.add).then_inc(s_k, 1)
            dve.wait_ge(s_k, 1)
            V.tensor_reduce(d1c[:], dwr[:], AX_X, ALU.add).then_inc(s_k, 1)
            dve.wait_ge(s_k, 2)
            V.tensor_scalar(d1c[:], d1c[:], b2r[:, 0:1], bdw[:, 0:1], ALU.mult, ALU.add).then_inc(s_k, 1)
            V.tensor_scalar(d1x[:], dwr[:, :, 0:3:2], b2r[:, 0:1], -1.0, ALU.mult, ALU.mult).then_inc(s_k, 1)
            dve.wait_ge(s_k, 4)

            def inverse_root(b, v, root, y, t):
                dve.wait_ge(s_sq, b + 1)
                V.reciprocal(y[:], root[:]).then_inc(s_pw, 1)
                dve.wait_ge(s_pw, 5 * b + 1)
                V.tensor_tensor(t[:], y[:], y[:], ALU.mult).then_inc(s_pw, 1)
                dve.wait_ge(s_pw, 5 * b + 2)
                V.tensor_tensor(t[:], t[:], v[:], ALU.mult).then_inc(s_pw, 1)
                dve.wait_ge(s_pw, 5 * b + 3)
                V.tensor_scalar(t[:], t[:], -0.5, 1.5, ALU.mult, ALU.add).then_inc(s_pw, 1)
                dve.wait_ge(s_pw, 5 * b + 4)
                V.tensor_tensor(y[:], y[:], t[:], ALU.mult).then_inc(s_pw, 1)
                dve.wait_ge(s_pw, 5 * b + 5)

            def x_stats(b, T, i, p, value):
                dve.wait_ge(s_xs[p], value)
                for j in range(4):
                    V.bn_stats(gst[:, bass.ds(T * 4 + j, 1), :].rearrange("p a s -> p (a s)"), xs[:, p, j]).then_inc(s_gs, 1)

            def first_stats(T, i, p, first, last):
                x_stats(0, T, i, p, at(0, i))
            steps(dve, first_stats)

            def batch(b, nxt):
                f0 = b * (GCH + ACH)
                m0 = b * SM
                dve.wait_ge(s_gs, 4 * NT * (b + 1))
                dve.wait_ge(s_cv, b * CV)
                V.memset(gb[:, 7, :], 0.0).then_inc(s_g7, 1)
                V.bn_aggr(mv[:], gst[:].rearrange("p k s -> p (k s)")).then_inc(s_f, 1)
                dve.wait_ge(s_m, m0 + 1)
                V.tensor_copy(mg[:], ps[:, 4, 0:1]).then_inc(s_f, 1)
                dve.wait_ge(s_f, f0 + 2)
                V.tensor_tensor(dev[:], mv[:, 0:1], mg[:], ALU.subtract).then_inc(s_f, 1)
                dve.wait_ge(s_f, f0 + 3)
                V.tensor_tensor(dv2[:], dev[:], dev[:], ALU.mult).then_inc(s_f, 1)
                dve.wait_ge(s_f, f0 + 4)
                V.tensor_tensor(dv2[:], dv2[:], mv[:, 1:2], ALU.add).then_inc(s_f, 1)
                dve.wait_ge(s_m, m0 + 2)
                V.tensor_scalar(vs[:], ps[:, 4, 1:2], GN_EPS, None, ALU.add).then_inc(s_f, 1)
                inverse_root(b, vs, sq, rs, nt)
                V.tensor_scalar(ws[:].rearrange("p g m -> p (g m)"), wqkv[:].rearrange("p g m -> p (g m)"),
                                rs[:, 0:1], None, ALU.mult).then_inc(s_ws, 1)
                dve.wait_ge(s_m, m0 + 3)
                V.tensor_tensor(bs[:], bqkv[:], ps[:, 4, 2:6], ALU.subtract).then_inc(s_bs, 1)


                def relu(T, J):
                    dve.wait_ge(s_cv, b * CV + 2 * T + J + 1)
                    dve.wait_ge(s_z1, b * NZB + 2 * T + J)
                    for q in range(2):
                        V.tensor_scalar(rb[:, q], ps[:, 2 + q, :], bc3[:, 0:1], 0.0, ALU.add, ALU.max).then_inc(s_r, 1)

                def write_z(t, slot, top, read):
                    dve.wait_ge(s_z1, b * NZB + t + 1)
                    dve.wait_ge(s_d, b * NZ + read)
                    if top:
                        V.tensor_scalar(zb[:, slot, 1:W + 1], ps[:, 4, :], keep0[:, 0:1], bc1[:, 1:2], ALU.mult,
                                        ALU.add).then_inc(s_z, 1)
                    else:
                        V.tensor_scalar(zb[:, slot, 1:W + 1], ps[:, 4, :], bc1[:, 0:1], None, ALU.add).then_inc(s_z, 1)

                def main(T, i, p, first, last):
                    n = b * NT + T
                    if not first:
                        write_z(2 * T - 1, (2 * p - 1) % 4, False, 0 if static(T, 2) else 2 * T - 4)
                    dve.wait_ge(s_qa, 3 * n + 1)
                    dve.wait_ge(s_tp, n)
                    V.tensor_tensor(qh[:], qb[:, 0:W:2], qb[:, 1:W:2], ALU.add).then_inc(s_h, 1)
                    dve.wait_ge(s_h, 3 * n + 1)
                    V.tensor_tensor(hq[:, p], qh[:], qb[:, 2:W + 2:2], ALU.add).then_inc(s_h, 1)
                    dve.wait_ge(s_qa, 3 * n + 2)
                    V.tensor_tensor(hk[:], kb[:, 0:W:2], kb[:, 1:W:2], ALU.max).then_inc(s_h, 1)
                    relu(T, 0)
                    write_z(2 * T, (2 * p) % 4, first, 0 if static(T, 2) else 2 * T - 2)
                    if nxt:
                        x_stats(b + 1, T, i, p, at(b + 1, i))
                    dve.wait_ge(s_tp, n + 1)
                    dve.wait_ge(s_sc, n)
                    V.tensor_scalar(qT[:].rearrange("p h m -> p (h m)"), ps[:, 6, 0:128], 1.0 / 9.0, None,
                                    ALU.mult).then_inc(s_te, 1)
                    V.tensor_reduce(kT[:].rearrange("p h (r c) -> p (h r) c", c=8),
                                    ps[:, 6, 128:384].rearrange("p (h r a c) -> p (h r) c a", h=2, a=2, c=8), AX_X,
                                    ALU.max).then_inc(s_te, 1)
                    relu(T, 1)
                    if not first:
                        d_stats(2 * T - 2)
                    if last:
                        write_z(2 * NT - 1, (2 * NT - 1) % 4, False, 2 * NT - 4)
                        dve.wait_ge(s_cv, b * CV + 2 * NT + 1)
                        dve.wait_ge(s_z1, b * NZB + 2 * NT)
                        V.tensor_scalar(rb[0:32, 0], ps[0:32, 2, :], bc3[0:32, 0:1], 0.0, ALU.add, ALU.max).then_inc(s_r, 1)
                        dve.wait_ge(s_d, b * NZ + 2 * NT - 2)
                        V.memset(zb[:, 0, :], 0.0).then_inc(s_zz, 1)
                        dve.wait_ge(s_zz, b + 1)
                        dve.wait_ge(s_z1, b * NZB + 2 * NT + 1)
                        V.tensor_scalar(zb[0:16, 0, 1:W + 1], ps[0:16, 4, :], bc1[0:16, 0:1], None,
                                        ALU.add).then_inc(s_z, 1)
                        d_stats(2 * NT - 2)

                def d_stats(t):
                    for q in range(2):
                        dve.wait_ge(s_de, b * NZ + t + q + 1)
                        V.bn_stats(dst2[:, bass.ds(b * NZ + t + q, 1), :].rearrange("p a s -> p (a s)"),
                                   db[:, q]).then_inc(s_dn, 1)

                steps(dve, main)

                g0 = f0 + GCH
                dve.wait_ge(s_sc, (b + 1) * NT)
                V.tensor_tensor(scm[:], ps[0:64, 7, 0:64], smask[:], ALU.mult).then_inc(s_f, 1)
                dve.wait_ge(s_m, m0 + 4)
                V.tensor_reduce(sc8[:], ps[0:8, 4, 0:64].rearrange("k (r q) -> k q r", q=8), AX_X, ALU.add).then_inc(s_f, 1)
                dve.wait_ge(s_f, g0 + 2)
                V.tensor_reduce(smx[:], sc8[:], AX_X, ALU.max).then_inc(s_f, 1)
                dve.wait_ge(s_f, g0 + 3)
                V.tensor_scalar(scd[:], sc8[:], smx[:, 0:1], None, ALU.subtract).then_inc(s_f, 1)
                dve.wait_ge(s_ex, b + 1)
                V.tensor_reduce(ssum[:], sce[:], AX_X, ALU.add).then_inc(s_f, 1)
                dve.wait_ge(s_f, g0 + 5)
                V.reciprocal(sinv[:], ssum[:]).then_inc(s_f, 1)
                dve.wait_ge(s_f, g0 + 6)
                V.tensor_scalar(sce[:], sce[:], sinv[:, 0:1], None, ALU.mult).then_inc(s_f, 1)
                dve.wait_ge(s_f, g0 + 7)
                V.tensor_copy(attn[:], bass_broadcast_rows(sce)).then_inc(s_f, 1)
                dve.wait_ge(s_m, m0 + 5)
                V.tensor_copy(mfac[:, bass.ds(b, 1), 0:16].rearrange("p a m -> p (a m)"), ps[:, 4, 64:80]).then_inc(s_f, 1)
                dve.wait_ge(s_m, m0 + 6)
                V.tensor_copy(mo[:], ps[0:16, 3, 0:128]).then_inc(s_f, 1)
                dve.wait_ge(s_m, m0 + 7)
                V.tensor_copy(mfac[:, bass.ds(b, 1), 16:48].rearrange("p a m -> p (a m)"), ps[:, 4, 96:128]).then_inc(s_f, 1)
                dve.wait_ge(s_f, g0 + 9)
                dw1_weights(b).then_inc(s_dw, 1)

                def dw1(T, i, p, first, last):
                    n = b * NT + T
                    for h in range(2):
                        dve.wait_ge(s_a1, 2 * n + h + 1)
                        v = 1 if first and h == 0 else 2 if last and h == 1 else 0
                        fix_columns(2 * p + h, v).then_inc(s_a1c, 1)
                    for h in range(2):
                        dve.wait_ge(s_a1e, 2 * n + h + 1)
                        V.bn_stats(dst1[:, bass.ds(b * NZ + T * 2 + h, 1), :].rearrange("p a s -> p (a s)"),
                                   yb[:, p, h, 0]).then_inc(s_a1n, 1)
                steps(dve, dw1)

            def bass_broadcast_rows(t):
                return t[:].unsqueeze(1).broadcast_to([8, 16, 8])

            def dw1_weights(b):
                m = mfac[:, bass.ds(b, 1), 0:16]
                return V.tensor_tensor(d1w[:].rearrange("p a r i -> p (a r) i"), td1[:].rearrange("p a r i -> p (a r) i"),
                                       m.broadcast_to([128, 48, 16]), ALU.mult)

            def fix_columns(bank, v):
                edge = ps[:, bank, 0:W:W - 1]
                return V.tensor_tensor(edge, edge, d1x[:, v, :], ALU.add)

            batches(dve, batch)

            fb = B * (GCH + ACH)
            dve.wait_ge(s_a1n, 2 * NT * B)
            dve.wait_ge(s_dn, NZ * B)
            for q, st in enumerate((dst1, dst2)):
                V.bn_aggr(mvb[:, q, :], st[:].rearrange("p k s -> p (k s)")).then_inc(s_f, 1)
            dve.wait_ge(s_m, B * SM + 2)
            V.tensor_copy(mgb[:], ps[:, 7, 4:6]).then_inc(s_f, 1)
            dve.wait_ge(s_f, fb + 3)
            V.tensor_tensor(devb[:], mvb[:, :, 0], mgb[:], ALU.subtract).then_inc(s_f, 1)
            dve.wait_ge(s_f, fb + 4)
            V.tensor_tensor(dvb2[:], devb[:], devb[:], ALU.mult).then_inc(s_f, 1)
            dve.wait_ge(s_f, fb + 5)
            V.tensor_tensor(dvb2[:], dvb2[:], mvb[:, :, 1], ALU.add).then_inc(s_f, 1)
            dve.wait_ge(s_m, B * SM + 3)
            V.tensor_scalar(vsb[:], ps[:, 7, 6:8], BN_EPS, None, ALU.add).then_inc(s_f, 1)
            inverse_root(B, vsb, sqb, rsb, ntb)
            V.tensor_tensor(ab[:, :, 0], rsb[:], bndw[:, :, 0], ALU.mult).then_inc(s_f, 1)
            dve.wait_ge(s_f, fb + 8)
            V.tensor_tensor(tmpb[:], mgb[:], ab[:, :, 0], ALU.mult).then_inc(s_f, 1)
            dve.wait_ge(s_f, fb + 9)
            V.tensor_tensor(ab[:, :, 1], bndw[:, :, 1], tmpb[:], ALU.subtract).then_inc(s_f, 1)
            V.tensor_tensor(x1c[:], b3r[:], ps[:, 7, 0:2], ALU.add).then_inc(s_f, 1)
            dve.wait_ge(s_f, fb + 10)
            V.tensor_scalar(bt[:], d1c[:], ab[:, 0, 0:1], ab[:, 0, 1:2], ALU.mult, ALU.add).then_inc(s_bn, 1)
            dve.wait_ge(s_f, fb + 11)

            def last_batch(b):
                if not static(b):
                    dve.wait_ge(s_fx, b * NT * 4)
                dw1_weights(b).then_inc(s_fw, 1)
                for e in range(2):
                    m3 = mfac[:, bass.ds(b, 1), 16 + e:48:2]
                    V.tensor_tensor(x1w[:, e].rearrange("p m r i -> p (m r) i"),
                                    rmask[:].rearrange("p m r -> p (m r)").unsqueeze(2).broadcast_to([128, 16, 16]),
                                    m3.broadcast_to([128, 16, 16]), ALU.mult).then_inc(s_fw, 1)

                def last_pass(T, i, p, first, last):
                    n = b * NT + T
                    for h in range(2):
                        dve.wait_ge(s_fa, 2 * n + h + 1)
                        v = 1 if first and h == 0 else 2 if last and h == 1 else 0
                        fix_columns(2 * p + h, v).then_inc(s_fc, 1)
                        if h == 0:
                            dve.wait_ge(s_x[p], at(B + b, i))
                        dve.wait_ge(s_fx, 4 * n + 2 * h + 2)
                        for e in range(2):
                            xt = xb[:, p, 2 * h + e]
                            op = V.scalar_tensor_tensor(xt, ps[:, 4 + 2 * h + e, :], x1c[:, e:e + 1], xt, ALU.add, ALU.add)
                        op.then_inc(s_ft, 1)
                    for h in range(2):
                        dve.wait_ge(s_ft, 2 * n + h + 1)
                        dve.wait_ge(s_fg, 4 * n + 2 * h + 2)
                        xt = xb[:, p, 2 * h:2 * h + 2].rearrange("p e w -> p (e w)")
                        V.tensor_tensor(xt, xt, yb[:, p, h].rearrange("p e w -> p (e w)"), ALU.add).then_inc(s_fo, 1)
                steps(dve, last_pass)
            last_batch(0)
            with dve.Fori(1, B) as b:
                last_batch(b)


def _toeplitz(rows_in, rows_out, shift, taps, dx):
    import numpy as np
    co, ci = taps.shape[:2]
    m = np.zeros((rows_in, ci, rows_out, co), taps.dtype)
    for a in range(rows_in):
        for o in range(rows_out):
            if 0 <= a - o + shift <= 2:
                m[a, :, o, :] = taps[:, :, a - o + shift, dx].T
    return m


def layouts(inp):
    import numpy as np
    g = {k: np.asarray(v) for k, v in inp.items()}
    L = lambda n: g["L0_conv_" + n]
    f = np.float32
    z = lambda *s: np.zeros(s, f)
    out = {"x": np.ascontiguousarray(g["x"].transpose(0, 2, 1, 3))}
    w = L("qkvl_w")[:, :, 0, 0]
    q = z(4, 32, 4, 128)
    for r in range(4):
        q[r, 16:32, 0, 32 * r:32 * r + 32] = w.T
        for h in range(3):
            for j in range(4):
                q[r, 0:16, 1 + h, 32 * j + 8 * r:32 * j + 8 * r + 8] = w[8 * h:8 * h + 8].T
    out["w_qkv"] = q.reshape(128, 4, 128)
    b = L("qkvl_b")
    out["b_qkv"] = np.stack([np.tile(b, 4)] + [np.tile(b[8 * h:8 * h + 8], 16) for h in range(3)], 1)
    c3 = L("conv3x3_w")
    out["w_c3"] = np.stack([_toeplitz(4, 2, s, c3, d).reshape(128, 64) for s in (0, -2, 2) for d in range(3)], 1)
    out["b_c3"] = np.stack([np.tile(L("conv3x3_b"), 4)] * 2, 1)
    c1 = L("conv1x1_w")[:, :, 0, 0]
    m = z(2, 4, 32, 4, 16)
    for v, order in enumerate(((0, 1, 2, 3), (2, 3, 0, 1))):
        for pos, l in enumerate(order):
            m[v, pos, :, l, :] = c1.T
    out["w_c1"] = np.ascontiguousarray(m.reshape(2, 128, 64).transpose(1, 0, 2))
    bz = np.tile(L("conv1x1_b"), 8)
    top = bz.copy()
    top[:16] = 0
    out["b_c1"] = np.stack([bz, top], 1)
    dw, dwb = L("dwc3x3_w"), L("dwc3x3_b")
    bn = np.stack([L("bn_gamma"), L("bn_beta")], 1)
    out["bn_dw"] = np.stack([np.tile(bn[e::2], (8, 1)) for e in range(2)], 1)
    diag = z(16, 16, 3, 3)
    for i in range(16):
        diag[i, i] = dw[2 * i + 1, 0]
    out["w_dw2"] = np.stack([_toeplitz(8, 4, s, diag, d).reshape(128, 64) for s in (0, -4, 4) for d in range(3)], 1)
    full = np.broadcast_to(dw[0::2], (16, 8, 3, 3))
    out["w_dw1"] = np.stack([_toeplitz(16, 2, -2 * m if h == 0 else -6 - 2 * m, full, d).reshape(128, 2, 16)
                             for h in range(2) for m in range(4) for d in range(3)], 1)
    s = np.broadcast_to(dw[0::2, 0].transpose(0, 2, 1)[None, :, None], (8, 16, 3, 3, 3)).copy()
    s[0, :, 1, :, 0] = 0
    s[7, :, 2, :, 2] = 0
    out["dw_sum"] = s.reshape(128, 3, 3, 3)
    b2 = L("conv1x1_2_b")
    out["b_2rep"] = np.tile(b2, 8).reshape(128, 1)
    out["b_dw"] = np.stack([np.tile(dwb[0::2], 8), np.tile(dwb[1::2], 8)], 1)
    out["w2t"] = np.ascontiguousarray(L("conv1x1_2_w")[:, :, 0, 0].T)
    w3 = L("conv1x1_3_w")[:, :, 0, 0]
    out["w3t"] = np.ascontiguousarray(w3.T)
    out["w3rep"] = np.stack([np.tile(w3[e::2].T, (1, 8)) for e in range(2)], 1)
    b3 = L("conv1x1_3_b")
    out["b3rep"] = np.stack([np.tile(b3[e::2], 8) for e in range(2)], 1)
    rm = z(16, 8, 8, 2)
    for h in range(2):
        for mq in range(4):
            for r in range(2):
                l = 2 * mq + r + 1 if h == 0 else 7 + 2 * mq + r
                rm[l, :, 4 * h + mq, r] = 1
    out["row_mask"] = rm.reshape(128, 8, 2)
    p = np.arange(128)
    out["gn_mix"] = ((p[:, None] % 32 // 2 == p[None] % 32 // 2) / 8).astype(f)
    out["bn_mix"] = ((p[:, None] % 16 == p[None] % 16) / 8).astype(f)
    out["ident"] = np.eye(128, dtype=f)
    ps = z(16, 8, 2, 8, 8)
    for c in range(8):
        for r in range(8):
            for a in (2 * r - 1, 2 * r, 2 * r + 1):
                if a >= 0:
                    ps[a, c, 0, r, c] = 1
        ps[15, c, 1, 0, c] = 1
    out["pool_sum"] = ps.reshape(128, 2, 64)
    a = np.arange(64)
    out["score_mask"] = (a[:, None] // 8 == a[None] // 8).astype(f)
    out["score_fold"] = (a[:, None] % 8 == np.arange(128)[None]).astype(f)
    k0 = np.ones((128, 1), f)
    k0[:16] = 0
    out["keep_first"] = k0
    return {k: np.ascontiguousarray(v, dtype=f) for k, v in out.items()}


def kernel(**inputs):
    import concourse.bacc as _bacc
    from concourse.bass_utils import run_bass_kernel_spmd as _run
    import numpy as np

    nc = _bacc.Bacc("TRN2", target_bir_lowering=False, num_devices=1)
    arrays = {f"in_{k}": v for k, v in layouts(inputs).items()}
    args = {k[3:]: nc.dram_tensor(k, v.shape, F32, kind="ExternalInput").ap() for k, v in arrays.items()}
    B, H = arrays["in_x"].shape[:2]
    out = nc.dram_tensor("out_0", (B, H, C, W), F32, kind="ExternalOutput").ap()
    v_dram = nc.dram_tensor("v_dram", (B, H + 2, 8, W), F32, kind="Internal").ap()
    d_dram = nc.dram_tensor("d_dram", (B, H, 16, W), F32, kind="Internal").ap()
    preact_kernel(nc, out=out, v_dram=v_dram, d_dram=d_dram, **args)
    r = _run(nc, [arrays], core_ids=[0])
    return np.ascontiguousarray(r.results[0]["out_0"].transpose(0, 2, 1, 3))
```

```python
from contextlib import ExitStack

import concourse.bass as bass
from concourse import mybir
from concourse.alu_op_type import AluOpType as ALU

F32 = mybir.dt.float32
F16 = mybir.dt.float16
ACT = mybir.ActivationFunctionType
AX_X = mybir.AxisListType.X

C = 32
W = 512
XR = 4
TR = 16
GN_EPS = BN_EPS = 1e-5

S_DATA = 2.0 ** 6
S_CONV = 2.0 ** 8
S_ATT = 2.0 ** 12
PARTS = ((0, 0), (0, 1), (1, 0))


def preact_kernel(nc, x, w_qkv, b_qkv, w_c3, b_c3, w_c1, b_c1, bn_dw, w_dw2, w_dw1, dw_sum, b_2rep, b_dw,
                  w2t, w3t, w3rep, b3rep, row_mask, gn_mix, bn_mix, ident, pool_sum, score_mask, score_fold,
                  out, v_dram, d_dram):
    B, H = x.shape[0], x.shape[1]
    NT = H // TR
    K = H // XR
    NZ = H // 8
    VR = v_dram.shape[1]
    assert NT % 4 == 0 and NT >= 12
    xrows = x.rearrange("b h c w -> (b h c) w")
    vrows = v_dram.rearrange("b h c q w -> (b h c) q w")
    drows = d_dram.rearrange("b h c w -> (b h c) w")
    xpair = x.rearrange("b h (i e) w -> (b h i) (e w)", e=2)
    opair = out.rearrange("b h (i e) w -> (b h i) (e w)", e=2)

    with ExitStack() as ctx:
        def sb(name, shape, dtype=F32):
            return ctx.enter_context(nc.sbuf_tensor("s_" + name, shape, dtype))

        def sem(name):
            return ctx.enter_context(nc.semaphore(name))

        wqkv = sb("wqkv", [128, 4, 128]);   bqkv = sb("bqkv", [128, 4])
        wc3 = sb("wc3", [128, 6, 64]);      bc3 = sb("bc3", [128, 2])
        wc1 = sb("wc1", [128, 2, 64]);      bc1 = sb("bc1", [128, 2])
        bndw = sb("bndw", [128, 2, 2]);     wd2 = sb("wd2", [128, 3, 64])
        td1 = sb("td1", [128, 24, 2, 16]);  dws = sb("dws", [128, 3, 3, 3])
        b2r = sb("b2r", [128, 1]);          bdw = sb("bdw", [128, 2])
        w2T = sb("w2T", [8, 16]);           w3T = sb("w3T", [16, 32])
        w3r = sb("w3r", [16, 2, 128]);      b3r = sb("b3r", [128, 2])
        b2c = sb("b2c", [16, 1])
        rmask = sb("rmask", [128, 8, 2]);   gmix = sb("gmix", [128, 128])
        bmix = sb("bmix", [128, 128]);      idn = sb("idn", [128, 128])
        psumw = sb("psumw", [128, 2, 64]);  smask = sb("smask", [64, 64])
        sfold = sb("sfold", [64, 128])
        wc3h = sb("wc3h", [128, 2, 6, 64], F16);   wd2h = sb("wd2h", [128, 2, 3, 64], F16)
        ws = sb("ws", [128, 4, 128]);       bs = sb("bs", [128, 4])
        mv = sb("mv", [128, 2]);            mg = sb("mg", [128, 1])
        dev = sb("dev", [128, 1]);          dv2 = sb("dv2", [128, 1]);  rs = sb("rs", [128, 1]);  vs = sb("vs", [128, 1]);  sq = sb("sq", [128, 1]);  nt = sb("nt", [128, 1])
        scm = sb("scm", [64, 64]);          sc8 = sb("sc8", [8, 8]);    scd = sb("scd", [8, 8])
        smx = sb("smx", [8, 1]);            sce = sb("sce", [8, 8]);    ssum = sb("ssum", [8, 1])
        sinv = sb("sinv", [8, 1]);          attn = sb("attn", [8, 16, 8])
        mo = sb("mo", [16, 128])
        mfac = sb("mfac", [128, B, 48])
        d1w = sb("d1w", [128, 24, 2, 16])
        x1w = sb("x1w", [128, 2, 8, 2, 16])
        d1wh = sb("d1wh", [128, 2, 24, 32], F16);   x1wh = sb("x1wh", [128, 2, 2, 8, 32], F16)
        d1c = sb("d1c", [128, 3]);          d1x = sb("d1x", [128, 3, 2])
        dwr = sb("dwr", [128, 3, 3])
        x1c = sb("x1c", [128, 2])
        ad1 = sb("ad1", [128, 1])
        ab = sb("ab", [128, 2, 2]);         bt = sb("bt", [128, 3]); mvb = sb("mvb", [128, 2, 2])
        mgb = sb("mgb", [128, 2]); devb = sb("devb", [128, 2]); dvb2 = sb("dvb2", [128, 2]); rsb = sb("rsb", [128, 2]); vsb = sb("vsb", [128, 2]); sqb = sb("sqb", [128, 2]); ntb = sb("ntb", [128, 2])
        tmpb = sb("tmpb", [128, 2]);  tmb2 = sb("tmb2", [128, 2])
        gst = sb("gst", [128, K, 6]);       dst1 = sb("dst1", [128, B * NZ, 6])
        dst2 = sb("dst2", [128, B * NZ, 6])
        xl = sb("xl", [128, 4, 4, W])
        xb = xl[:, 0:2]
        xs = xl[:, 2:4]
        dl = sb("dl", [128, 4, 2, W])
        gf = dl[:, 0:2].rearrange("p t h w -> p (t h) w")
        gb = sb("gb", [128, 8, 2, W + 2], F16)
        va = gb[:].rearrange("p (t h) q w -> p t h q w", h=2)
        gB = sb("gB", [128, 4, 2, W + 2], F16)
        zB = sb("zB", [128, 2, 2, W + 2], F16)
        rb = sb("rb", [128, 2, W])
        zb = sb("zb", [128, 4, 2, W + 2], F16)
        db = sb("db", [128, 2, W])
        qb = sb("qb", [128, W + 2]);        kb = sb("kb", [128, W])
        vb = sb("vb", [128, 2, W]);         vh = sb("vh", [128, 2, 2, W], F16)
        qh = sb("qh", [128, W // 2]);       hq = sb("hq", [128, 2, W // 2]);  hk = sb("hk", [128, W // 2])
        qT = sb("qT", [128, 2, 64]);        kT = sb("kT", [128, 2, 64])
        yb = sb("yb", [128, 2, 2, 2, W])
        ps = ctx.enter_context(nc.psum_tensor("ps", [128, 8, W], F32))

        s_cst = sem("consts_loaded")
        s_x = [sem("x_loaded_even"), sem("x_loaded_odd")]
        s_xs = [sem("xs_loaded_even"), sem("xs_loaded_odd")]
        s_va = [sem("va_loaded_even"), sem("va_loaded_odd")]
        s_lv = [sem("last_v_loaded_%d" % r) for r in range(4)]
        s_ld = [sem("last_d_loaded_%d" % r) for r in range(4)]
        s_lx = [sem("last_x_loaded_%d" % r) for r in range(4)]
        s_vst = [sem("v_stored_even"), sem("v_stored_odd")]
        s_dst = [sem("d_stored_even"), sem("d_stored_odd")]
        s_ost = [sem("out_stored_%d" % r) for r in range(4)]
        s_zv = sem("v_borders_stored")
        s_pad = sem("pads_zeroed")
        s_g7 = sem("above_image_zeroed")
        s_q2 = sem("block_product_done"); s_g = sem("g_written"); s_gh = sem("g_high_written"); s_gl = sem("g_low_written"); s_cv = sem("conv_done")
        s_r = sem("relu_written"); s_z1 = sem("conv1x1_done"); s_zh = sem("z_high_written"); s_z = sem("z_low_written"); s_top = sem("row_above_masked")
        s_gc = [sem("g_shifted_even"), sem("g_shifted_odd")];   s_zc = sem("z_shifted")
        s_q = sem("qkv_product_done"); s_qa = sem("qkv_written"); s_vh = sem("v_high_written"); s_vl = sem("v_low_written")
        s_h = sem("pool_rows_done"); s_hs = sem("pool_partial_done")
        s_tp = sem("pooled_transposed"); s_te = sem("pooled_copied"); s_sc = sem("scores_added")
        s_d = sem("dw_done"); s_de = sem("dw_written"); s_dn = sem("dw_stats_done")
        s_gs = sem("x_stats_done")
        s_f = sem("dve_chain"); s_k = sem("d1_constants"); s_pw = sem("rstd_steps"); s_sq = sem("root_written"); s_zz = sem("below_image_zeroed"); s_m = sem("small_product_done"); s_ws = sem("weights_scaled")
        s_bs = sem("bias_ready"); s_ex = sem("exp_done"); s_dw = sem("dw1_weights_ready")
        s_wsp = sem("product_weights_split")
        s_a1 = sem("dw1_done"); s_a1c = sem("dw1_columns_fixed"); s_a1e = sem("dw1_written")
        s_a1n = sem("dw1_stats_done")
        s_fa = sem("last_dw1_done"); s_fc = sem("last_columns_fixed"); s_fx = sem("last_x1o_done")
        s_fg = sem("last_gelu_done"); s_ft = sem("last_residual_done"); s_fo = sem("last_sum_done")
        s_bn = sem("bn_ready"); s_x1p = sem("last_weight_products"); s_fw = sem("last_weights_ready")

        small = [(w_qkv, wqkv), (b_qkv, bqkv), (w_c3, wc3), (b_c3, bc3), (w_c1, wc1), (b_c1, bc1), (bn_dw, bndw),
                 (w_dw2, wd2), (w_dw1, td1), (dw_sum, dws), (b_2rep, b2r), (b_dw, bdw), (w2t, w2T), (w3t, w3T),
                 (w3rep, w3r), (b3rep, b3r), (row_mask, rmask), (gn_mix, gmix), (bn_mix, bmix), (ident, idn),
                 (pool_sum, psumw), (score_mask, smask), (score_fold, sfold)]
        NCONST = 16 * (len(small) + 1)

        block = ctx.enter_context(nc.Block())

        def batches(eng, body):
            body(0, True)
            with eng.Fori(1, B - 1) as b:
                body(b, True)
            body(B - 1, False)

        def steps(eng, body):
            body(0, 0, 0, True, False)
            body(1, 0, 1, False, False)
            with eng.Fori(1, NT // 2 - 1) as i:
                body(i * 2, i, 0, False, False)
                body(i * 2 + 1, i, 1, False, False)
            body(NT - 2, NT // 2 - 1, 0, False, False)
            body(NT - 1, NT // 2 - 1, 1, False, True)

        def steps4(eng, body):
            for r in range(4):
                body(r, 0, r, r == 0, False)
            with eng.Fori(1, NT // 4 - 1) as i:
                for r in range(4):
                    body(i * 4 + r, i, r, False, False)
            for r in range(4):
                body(NT - 4 + r, NT // 4 - 1, r, False, r == 3)

        def static(v, below=1):
            return isinstance(v, int) and v < below

        NP = NT // 2
        NF = NT // 4
        CV = 2 * NT + 1
        NRL = 4 * NT + 1
        NZB = 2 * NT + 1
        SM = 7
        GCH, ACH = 6, 11

        def at(b, i):
            return 16 * (b * NP + i) + 16

        @block.sync
        def _(sp):
            for src, dst in small:
                sp.dma_start(dst[:], src).then_inc(s_cst, 16)
            sp.dma_start(b2c[:], b_2rep[0:16, :]).then_inc(s_cst, 16)
            sp.wait_ge(s_pad, 3)
            for b in range(B):
                sp.dma_start(vrows[b * VR * 8:b * VR * 8 + 8], va[0:8, 0, 0, :, 0:W]).then_inc(s_zv, 16)
                sp.dma_start(vrows[(b * VR + H + 1) * 8:(b + 1) * VR * 8], va[0:8, 0, 0, :, 0:W]).then_inc(s_zv, 16)

            def load_x(b, T, p):
                sp.dma_start(xb[:, p], xrows[bass.ds((b * H + T * TR) * C, TR * C), :]
                             .rearrange("(k p) w -> p k w", p=128)).then_inc(s_x[p], 16)

            def load_stats(b, T, p):
                sp.dma_start(xs[:, p], xrows[bass.ds((b * H + T * TR) * C, TR * C), :]
                             .rearrange("(k p) w -> p k w", p=128)).then_inc(s_xs[p], 16)

            def first_stats(T, i, p, first, last):
                if not static(T, 2):
                    sp.wait_ge(s_gs, 4 * (T - 1))
                load_stats(0, T, p)
            steps(sp, first_stats)

            def batch(b, nxt):
                def shift_g(J, s):
                    sp.dma_start(gB[0:64, 2 * J], gb[64:128, (s - 1) % 8]).then_inc(s_gc[J], 16)
                    sp.dma_start(gB[0:64, 2 * J + 1], gb[64:128, s]).then_inc(s_gc[J], 16)
                    sp.dma_start(gB[64:128, 2 * J:2 * J + 2], gb[0:64, s:s + 2]).then_inc(s_gc[J], 16)

                def shift_z(u, s):
                    sp.wait_ge(s_z, b * NZB + 2 * u + 2)
                    sp.dma_start(zB[0:64, 0:2], zb[64:128, s:s + 2]).then_inc(s_zc, 16)
                    sp.dma_start(zB[64:128, 0], zb[0:64, s + 1]).then_inc(s_zc, 16)

                def shift_z_next(u, s):
                    sp.wait_ge(s_z, b * NZB + 2 * u + 3)
                    sp.dma_start(zB[64:128, 1], zb[0:64, (s + 2) % 4]).then_inc(s_zc, 16)

                def store_d(u):
                    for q in range(2):
                        t = 2 * u + q
                        sp.wait_ge(s_de, b * NZ + t + 1)
                        if q == 0:
                            sp.dma_start(drows[bass.ds((b * H + t * 8) * 16, 128), :], db[:, q]).then_inc(s_dst[q], 16)
                        else:
                            sp.dma_start(drows[bass.ds((b * H + t * 8) * 16, 64), :], db[64:128, q]).then_inc(s_dst[q], 16)
                            sp.dma_start(drows[bass.ds((b * H + t * 8 + 4) * 16, 64), :], db[0:64, q]).then_inc(s_dst[q], 16)

                def main(T, i, p, first, last):
                    n = b * NT + T
                    if nxt:
                        sp.wait_ge(s_gs, 4 * ((b + 1) * NT + T - 1))
                        load_stats(b + 1, T, p)
                    sp.wait_ge(s_gl, b * K + 4 * T + 4)
                    shift_g(1, 4 * p + 2)
                    if not first:
                        shift_z(T - 1, (2 * p - 2) % 4)
                    if not static(T, 2):
                        store_d(T - 2)
                    sp.wait_ge(s_vl, n + 1)
                    sp.dma_start(vrows[bass.ds((b * VR + 1 + T * TR) * 8, 128)], vh[:, p]).then_inc(s_vst[p], 16)
                    if not first:
                        shift_z_next(T - 1, (2 * p - 2) % 4)
                    if not (isinstance(T, int) and T >= NT - 2):
                        sp.wait_ge(s_q, 3 * (n + 1))
                        load_x(b, T + 2, p)
                    if not last:
                        sp.wait_ge(s_gl, b * K + 4 * T + 6)
                        shift_g(0, (4 * p + 4) % 8)

                sp.wait_ge(s_gl, b * K + 2)
                shift_g(0, 0)
                steps(sp, main)
                shift_z(NT - 1, 2)
                store_d(NT - 2)
                shift_z_next(NT - 1, 2)
                store_d(NT - 1)

                if nxt:
                    sp.wait_ge(s_q, 3 * (b + 1) * NT)
                    for q in range(2):
                        load_x(b + 1, q, q)
                sp.wait_ge(s_cv, (b + 1) * CV)
                for q in range(2):
                    sp.wait_ge(s_vst[q], at(b, NP - 1))


                def dw1(T, i, p, first, last):
                    if not static(T, 2):
                        sp.wait_ge(s_a1, 2 * (b * NT + T) - 2)
                    load_va(b, T, p, s_va[p])
                steps(sp, dw1)

            def load_va(b, T, slot, loaded):
                for h in range(2):
                    sp.dma_start(va[:, slot, h, :, 1:W + 1],
                                 vrows[bass.ds((b * VR + T * TR + 2 * h) * 8, 128)]).then_inc(loaded, 16)

            sp.wait_ge(s_zv, 32 * B)
            for q in range(2):
                load_x(0, q, q)
            batches(sp, batch)
            sp.wait_ge(s_a1, 2 * NT * B)
            sp.wait_ge(s_q, 3 * B * NT)
            sp.wait_ge(s_dst[0], B * NT * 16)
            sp.wait_ge(s_dst[1], B * NT * 32)

            def last_batch(b):
                def last_pass(T, i, r, first, last):
                    if not (static(b) and static(T, 4)):
                        sp.wait_ge(s_ost[r], (b * NF + i) * 32)
                    load_va(b, T, r, s_lv[r])
                    sp.dma_start(dl[:, r], drows[bass.ds((b * H + T * TR) * 16, 256), :]
                                 .rearrange("(h p) w -> p h w", p=128)).then_inc(s_ld[r], 16)
                    sp.dma_start(xl[:, r].rearrange("p (h e) w -> p h (e w)", h=2),
                                 xpair[bass.ds((b * H + T * TR) * 16, 256), :]
                                 .rearrange("(h p) w -> p h w", p=128)).then_inc(s_lx[r], 16)
                steps4(sp, last_pass)
            last_batch(0)
            with sp.Fori(1, B) as b:
                last_batch(b)

        @block.gpsimd
        def _(pool):
            pool.memset(gb[:], 0.0).then_inc(s_pad, 1)
            pool.memset(zb[:], 0.0).then_inc(s_pad, 1)
            pool.memset(qb[:], 0.0).then_inc(s_pad, 1)

            def last_batch(b):
                def last_pass(T, i, r, first, last):
                    n = b * NT + T
                    for h in range(2):
                        pool.wait_ge(s_fo, 2 * n + h + 1)
                        pool.dma_start(opair[bass.ds((b * H + T * TR + 8 * h) * 16, 128), :],
                                       xl[:, r, 2 * h:2 * h + 2].rearrange("p e w -> p (e w)")).then_inc(s_ost[r], 16)
                steps4(pool, last_pass)
            last_batch(0)
            with pool.Fori(1, B) as b:
                last_batch(b)
            for r in range(4):
                pool.wait_ge(s_ost[r], B * NF * 32)

        @block.tensor
        def _(pe):
            mm = nc.tensor.matmul
            pe.wait_ge(s_cst, NCONST)
            pe.wait_ge(s_pad, 3)
            pe.wait_ge(s_k, 11)

            def batch(b, nxt):
                pe.wait_ge(s_a1e, 2 * NT * b)
                pe.wait_ge(s_f, b * (GCH + ACH) + 1)
                mm(ps[:, 4, 0:1], gmix[:], mv[:, 0:1], start=True, stop=True).then_inc(s_m, 1)
                pe.wait_ge(s_f, b * (GCH + ACH) + 5)
                mm(ps[:, 4, 1:2], gmix[:], dv2[:], start=True, stop=True).then_inc(s_m, 1)
                pe.wait_ge(s_ws, b + 1)
                for g in range(4):
                    last = mm(ps[:, 4, 2 + g:3 + g], ws[:, g, :], mg[:], start=True, stop=True)
                last.then_inc(s_m, 1)

                def product(k, p, j):
                    if not static(k, 2):
                        pe.wait_ge(s_g, b * K + k - 1)
                    mm(ps[:, j % 2, :], ws[:, 0, :], xb[:, p, j], start=True, stop=True).then_inc(s_q2, 1)

                def qkv(n, part, p, bank):
                    for j in range(4):
                        last = mm(ps[32 * j:32 * j + 32, bank, :], ws[:, 1 + part, 0:32], xb[:, p, j], start=True, stop=True)
                    return last

                def conv(lists):
                    last = None
                    for step in range(max(len(l) for l in lists)):
                        for l in lists:
                            if step < len(l):
                                o, w, m, st, sp_ = l[step]
                                last = mm(o, w, m, start=st, stop=sp_)
                    return last

                def taps(o, terms):
                    return [(o, w, m, i == 0, i == len(terms) - 1) for i, (w, m) in enumerate(terms)]

                def conv3x3(p, J):
                    s0 = 4 * p + 2 * J
                    def terms(tile):
                        return [(wc3h[:, u, d, :], tile[:, v, d:d + W]) for u, v in PARTS for d in range(3)]
                    left = taps(ps[0:64, 2, :], terms(gB[:, 2 * J])) + taps(ps[0:64, 3, :], terms(gb[:, s0 + 1]))
                    right = taps(ps[64:128, 2, :], terms(gb[:, s0])) + taps(ps[64:128, 3, :], terms(gB[:, 2 * J + 1]))
                    return conv([left, right])

                def conv1x1():
                    mm(ps[0:64, 4, :], wc1[:, 0, :], rb[:, 0], start=True, stop=True)
                    mm(ps[64:128, 4, :], wc1[:, 1, :], rb[:, 1], start=True, stop=True).then_inc(s_z1, 1)

                def dw2(s0):
                    def terms(tile):
                        return [(wd2h[:, u, d, :], tile[:, v, d:d + W]) for u, v in PARTS for d in range(3)]
                    left = taps(ps[0:64, 5, :], terms(zb[:, s0])) + taps(ps[0:64, 6, :], terms(zB[:, 1]))
                    right = taps(ps[64:128, 5, :], terms(zB[:, 0])) + taps(ps[64:128, 6, :], terms(zb[:, s0 + 1]))
                    return conv([left, right])

                def dw2_pair(u, s0):
                    pe.wait_ge(s_zc, 48 * (b * NT + u + 1))
                    dw2(s0).then_inc(s_d, 2)

                pe.wait_ge(s_bs, b + 1)
                pe.wait_ge(s_x[0], at(b, 0))
                pe.wait_ge(s_g, b * K)
                product(0, 0, 0)
                product(1, 0, 1)
                pe.wait_ge(s_g7, b + 1)

                def main(T, i, p, first, last):
                    n = b * NT + T
                    product(4 * T + 2, p, 2)
                    product(4 * T + 3, p, 3)
                    if not first:
                        pe.wait_ge(s_r, b * NRL + 4 * T)
                        pe.wait_ge(s_z, b * NZB + 2 * T - 1)
                        conv1x1()
                    if first:
                        pe.wait_ge(s_de, b * NZ)
                    else:
                        if not static(T, 2):
                            pe.wait_ge(s_de, b * NZ + 2 * T - 2)
                    qkv(n, 0, p, 5).then_inc(s_q, 1)
                    qkv(n, 1, p, 6).then_inc(s_q, 1)
                    pe.wait_ge(s_gc[0], 48 * (n + 1))
                    conv3x3(p, 0).then_inc(s_cv, 1)
                    pe.wait_ge(s_qa, 3 * n + 1)
                    v = qkv(n, 2, p, 5)
                    v.then_inc(s_q, 1)
                    if not last:
                        pe.wait_ge(s_x[1 - p], at(b, i + p))
                        product(4 * T + 4, 1 - p, 0)
                        product(4 * T + 5, 1 - p, 1)
                    pe.wait_ge(s_r, b * NRL + 4 * T + 2)
                    if not first:
                        pe.wait_ge(s_z, b * NZB + 2 * T)
                    else:
                        pe.wait_ge(s_top, b + 1)
                    conv1x1()
                    pe.wait_ge(s_h, 3 * (n + 1))
                    pe.wait_ge(s_qa, 3 * n + 2)
                    for h in range(2):
                        cols = slice(128 * h, 128 * h + 128)
                        mm(ps[:, 6, 64 * h:64 * h + 64], hq[:, p, cols], psumw[:, 0, :], start=(h == 0), stop=first,
                           skip_group_check=True)
                        if not first:
                            mm(ps[:, 6, 64 * h:64 * h + 64], hq[:, 1 - p, cols], psumw[:, 1, :], start=False, stop=True,
                               skip_group_check=True)
                    for h in range(2):
                        cols = slice(128 * h, 128 * h + 128)
                        tk = mm(ps[:, 6, 128 + 128 * h:256 + 128 * h], hk[:, cols], idn[:], start=False, stop=True,
                                skip_group_check=True)
                    tk.then_inc(s_tp, 1)
                    pe.wait_ge(s_gc[1], 48 * (n + 1))
                    conv3x3(p, 1).then_inc(s_cv, 1)
                    pe.wait_ge(s_qa, 3 * n + 3)
                    pe.wait_ge(s_te, 2 * n + 2)
                    if not first:
                        dw2_pair(T - 1, (2 * p - 2) % 4)
                    for h in range(2):
                        sc = mm(ps[0:64, 7, 0:64], kT[:, h, :], qT[:, h, :], start=(first and h == 0),
                                stop=(last and h == 1), skip_group_check=True)
                    sc.then_inc(s_sc, 1)
                steps(pe, main)

                pe.wait_ge(s_r, b * NRL + 4 * NT)
                pe.wait_ge(s_z, b * NZB + 2 * NT - 1)
                conv1x1()
                conv([taps(ps[0:64, 2, :], [(wc3h[:, u, 3 + d, :], gb[:, 7, v, d:d + W]) for u, v in PARTS
                                              for d in range(3)])]).then_inc(s_cv, 1)
                pe.wait_ge(s_r, b * NRL + 4 * NT + 1)
                pe.wait_ge(s_z, b * NZB + 2 * NT)
                mm(ps[0:64, 4, :], wc1[0:32, 0, :], rb[0:32, 0], start=True, stop=True).then_inc(s_z1, 1)
                pe.wait_ge(s_de, b * NZ + 2 * NT - 2)
                dw2_pair(NT - 1, (2 * NT - 2) % 4)

                pe.wait_ge(s_f, b * (GCH + ACH) + GCH + 1)
                mm(ps[:, 4, 0:64], sfold[:], scm[:], start=True, stop=True).then_inc(s_m, 1)
                pe.wait_ge(s_f, b * (GCH + ACH) + GCH + 8)
                mm(ps[:, 4, 64:80], attn[:].rearrange("i l j -> i (l j)"), w2T[:], start=True, stop=True).then_inc(s_m, 1)
                mm(ps[0:16, 3, 0:128], w2T[:], attn[:].rearrange("i l j -> i (l j)"), start=True, stop=True).then_inc(s_m, 1)
                pe.wait_ge(s_f, b * (GCH + ACH) + GCH + 10)
                mm(ps[:, 4, 96:128], mo[:], w3T[:], start=True, stop=True).then_inc(s_m, 1)

                pe.wait_ge(s_dw, b + 1)

                def dw1(T, i, p, first, last):
                    n = b * NT + T
                    pe.wait_ge(s_va[p], 2 * at(b, i))
                    for h in range(2):
                        if not static(T, 2):
                            pe.wait_ge(s_a1e, 2 * n + h - 3)
                        dwconv1(mm, 2 * p + h, p, h).then_inc(s_a1, 1)
                steps(pe, dw1)

            def dwconv1(mm, bank, slot, h):
                for i, (u, v) in enumerate(PARTS):
                    for d in range(3):
                        for m in range(4):
                            last = mm(ps[32 * m:32 * m + 32, bank, :], d1wh[:, u, (4 * h + m) * 3 + d, :],
                                      va[:, slot, h, v, d:d + W], start=(i == 0 and d == 0), stop=(i == 2 and d == 2))
                return last

            batches(pe, batch)

            pe.wait_ge(s_a1e, 2 * NT * B)
            for e in range(2):
                last = mm(ps[:, 7, e:e + 1], w3r[:, e, :], b2c[:], start=True, stop=True)
            last.then_inc(s_m, 1)
            pe.wait_ge(s_f, B * (GCH + ACH) + 2)
            mm(ps[:, 7, 4:6], bmix[:], mvb[:, :, 0], start=True, stop=True).then_inc(s_m, 1)
            pe.wait_ge(s_f, B * (GCH + ACH) + 6)
            mm(ps[:, 7, 6:8], bmix[:], dvb2[:], start=True, stop=True).then_inc(s_m, 1)

            def last_batch(b):
                pe.wait_ge(s_fw, b + 1)

                def last_pass(T, i, r, first, last):
                    n = b * NT + T
                    p = r % 2
                    pe.wait_ge(s_lv[r], 32 * (b * NF + i) + 32)
                    for h in range(2):
                        if not (static(b) and static(T, 2)):
                            pe.wait_ge(s_fg, 4 * n + 2 * h - 6)
                        dwconv1(mm, 2 * p + h, r, h).then_inc(s_fa, 1)
                        if not (static(b) and first):
                            pe.wait_ge(s_ft, 2 * n + h - 1)
                        for e in range(2):
                            for i, (u, v) in enumerate(PARTS):
                                for m in range(4):
                                    o = mm(ps[32 * m:32 * m + 32, 4 + 2 * h + e, :], x1wh[:, u, e, 4 * h + m, :],
                                           va[:, r, h, v, 1:1 + W], start=(i == 0), stop=(i == 2))
                            o.then_inc(s_fx, 1)
                steps4(pe, last_pass)
            last_batch(0)
            with pe.Fori(1, B) as b:
                last_batch(b)

        @block.scalar
        def _(act):
            fn = nc.scalar.activation
            act.wait_ge(s_cst, NCONST)
            act.wait_ge(s_pad, 3)

            def batch(b, nxt):
                act.wait_ge(s_f, b * (GCH + ACH) + 6)
                fn(sq[:], vs[:], ACT.Sqrt).then_inc(s_sq, 1)
                act.wait_ge(s_bs, b + 1)
                act.wait_ge(s_k, 11)

                def main(T, i, p, first, last):
                    n = b * NT + T

                    def gelu(j):
                        act.wait_ge(s_q2, b * K + 4 * T + j + 1)
                        act.wait_ge(s_gl, b * K if static(T, 2) and 4 * T + j < 4 else b * K + 4 * T + j - 3)
                        fn(gf[:, j % 4], ps[:, j % 2, :], ACT.Gelu, bias=bs[:, 0:1]).then_inc(s_g, 1)

                    def high(j):
                        slot = (4 * p + j) % 8
                        act.wait_ge(s_g, b * K + 4 * T + j + 1)
                        if static(T, 2) and 4 * T + j < 7:
                            act.wait_ge(s_cv, b * CV)
                        else:
                            act.wait_ge(s_cv, b * CV + 2 * T + (j - 5) // 2)
                        fn(gb[:, slot, 0, 1:W + 1], gf[:, j % 4], ACT.Copy, scale=S_DATA).then_inc(s_gh, 1)

                    def high_z(t, slot, top, read):
                        act.wait_ge(s_z1, b * NZB + t + 1)
                        act.wait_ge(s_d, b * NZ + read)
                        fn(zb[:, slot, 0, 1:W + 1], ps[:, 4, :], ACT.Identity, bias=bc1[:, top:top + 1]).then_inc(s_zh, 1)

                    def gelu_qkv(part, dst):
                        act.wait_ge(s_q, 3 * n + part + 1)
                        fn(dst, ps[:, 5 + part % 2, :], ACT.Gelu, bias=bs[:, 1 + part:2 + part]).then_inc(s_qa, 1)

                    if first:
                        gelu(0)
                        gelu(1)
                        high(0)
                        high(1)
                    gelu(2)
                    gelu(3)
                    high(2)
                    high(3)
                    if not first:
                        high_z(2 * T - 1, (2 * p - 1) % 4, 0, 0 if static(T, 2) else 2 * T - 4)
                    act.wait_ge(s_h, 3 * n)
                    gelu_qkv(0, qb[:, 1:W + 1])
                    gelu_qkv(1, kb[:])
                    act.wait_ge(s_vl, b * NT if static(T, 2) else n - 1)
                    gelu_qkv(2, vb[:, p])
                    if not last:
                        gelu(4)
                        gelu(5)
                    act.wait_ge(s_qa, 3 * n + 3)
                    act.wait_ge(s_vst[p], 16 * (b * NP + i))
                    fn(vh[:, p, 0], vb[:, p], ACT.Copy, scale=S_DATA).then_inc(s_vh, 1)
                    high_z(2 * T, (2 * p) % 4, 1 if first else 0, 0 if static(T, 2) else 2 * T - 2)
                    if not last:
                        high(4)
                        high(5)
                    if not first:
                        write_d(T - 1, static(T, 2))
                    if last:
                        high_z(2 * NT - 1, (2 * NT - 1) % 4, 0, 2 * NT - 4)
                        act.wait_ge(s_z1, b * NZB + 2 * NT + 1)
                        act.wait_ge(s_zz, b + 1)
                        fn(zb[0:16, 0, 0, 1:W + 1], ps[0:16, 4, :], ACT.Identity, bias=bc1[0:16, 0:1]).then_inc(s_zh, 1)
                        write_d(NT - 1, False)

                def write_d(u, head):
                    act.wait_ge(s_d, b * NZ + 2 * u + 2)
                    for q in range(2):
                        act.wait_ge(s_dn, b * NZ if head else b * NZ + 2 * u + q - 1)
                        act.wait_ge(s_dst[q], (16 if q == 0 else 32) * (b * NT + u))
                        fn(db[:, q], ps[:, 5 + q, :], ACT.Identity, bias=bdw[:, 1:2],
                           scale=1 / (S_DATA * S_CONV)).then_inc(s_de, 1)

                steps(act, main)

                act.wait_ge(s_f, b * (GCH + ACH) + GCH + 4)
                fn(sce[:], scd[:], ACT.Exp).then_inc(s_ex, 1)

                def dw1(T, i, p, first, last):
                    n = b * NT + T
                    for h in range(2):
                        act.wait_ge(s_a1c, 2 * n + h + 1)
                        act.wait_ge(s_a1n, 2 * NT * b if static(T, 2) else 2 * n + h - 3)
                        v = 1 if first and h == 0 else 2 if last and h == 1 else 0
                        fn(yb[:, p, h, 0], ps[:, 2 * p + h, :], ACT.Identity, bias=d1c[:, v:v + 1],
                           scale=1 / (S_DATA * S_ATT)).then_inc(s_a1e, 1)
                steps(act, dw1)
            batches(act, batch)

            act.wait_ge(s_f, B * (GCH + ACH) + 7)
            fn(sqb[:], vsb[:], ACT.Sqrt).then_inc(s_sq, 1)
            act.wait_ge(s_bn, 1)

            def last_batch(b):
                def last_pass(T, i, r, first, last):
                    n = b * NT + T
                    p = r % 2
                    act.wait_ge(s_ld[r], 16 * (b * NF + i) + 16)
                    for h in range(2):
                        act.wait_ge(s_fc, 2 * n + h + 1)
                        if not (static(b) and static(T, 2)):
                            act.wait_ge(s_fo, 2 * n + h - 3)
                        v = 1 if first and h == 0 else 2 if last and h == 1 else 0
                        fn(yb[:, p, h, 0], ps[:, 2 * p + h, :], ACT.Gelu, bias=bt[:, v:v + 1],
                           scale=ad1[:, 0:1]).then_inc(s_fg, 1)
                        fn(yb[:, p, h, 1], dl[:, r, h], ACT.Gelu, bias=ab[:, 1, 1:2],
                           scale=ab[:, 1, 0:1]).then_inc(s_fg, 1)
                steps4(act, last_pass)
            last_batch(0)
            with act.Fori(1, B) as b:
                last_batch(b)

        @block.vector
        def _(dve):
            V = nc.vector
            dve.wait_ge(s_cst, NCONST)
            dve.wait_ge(s_pad, 3)

            V.tensor_reduce(dwr[:].rearrange("p v d -> p (v d)"), dws[:].rearrange("p v d y -> p (v d) y"), AX_X,
                            ALU.add).then_inc(s_k, 1)
            dve.wait_ge(s_k, 1)
            V.tensor_reduce(d1c[:], dwr[:], AX_X, ALU.add).then_inc(s_k, 1)
            dve.wait_ge(s_k, 2)
            V.tensor_scalar(d1c[:], d1c[:], b2r[:, 0:1], bdw[:, 0:1], ALU.mult, ALU.add).then_inc(s_k, 1)
            V.tensor_scalar(d1x[:], dwr[:, :, 0:3:2], b2r[:, 0:1], -S_DATA * S_ATT, ALU.mult, ALU.mult).then_inc(s_k, 1)
            for j, (w, parts) in enumerate(((wc3, wc3h), (wd2, wd2h))):
                V.tensor_scalar(parts[:, 0], w[:], S_CONV, None, ALU.mult).then_inc(s_k, 1)
                dve.wait_ge(s_k, 5 + 2 * j)
                V.scalar_tensor_tensor(parts[:, 1], w[:], S_CONV, parts[:, 0], ALU.mult, ALU.subtract).then_inc(s_k, 1)
            V.tensor_scalar(bc3[:], bc3[:], S_DATA * S_CONV, None, ALU.mult).then_inc(s_k, 1)
            V.tensor_scalar(wc1[:], wc1[:], 1 / S_CONV, None, ALU.mult).then_inc(s_k, 1)
            V.tensor_scalar(bc1[:], bc1[:], S_DATA, None, ALU.mult).then_inc(s_k, 1)
            dve.wait_ge(s_k, 11)

            def inverse_root(b, v, root, y, t):
                dve.wait_ge(s_sq, b + 1)
                V.reciprocal(y[:], root[:]).then_inc(s_pw, 1)
                dve.wait_ge(s_pw, 5 * b + 1)
                V.tensor_tensor(t[:], y[:], y[:], ALU.mult).then_inc(s_pw, 1)
                dve.wait_ge(s_pw, 5 * b + 2)
                V.tensor_tensor(t[:], t[:], v[:], ALU.mult).then_inc(s_pw, 1)
                dve.wait_ge(s_pw, 5 * b + 3)
                V.tensor_scalar(t[:], t[:], -0.5, 1.5, ALU.mult, ALU.add).then_inc(s_pw, 1)
                dve.wait_ge(s_pw, 5 * b + 4)
                V.tensor_tensor(y[:], y[:], t[:], ALU.mult).then_inc(s_pw, 1)
                dve.wait_ge(s_pw, 5 * b + 5)

            def x_stats(b, T, i, p, value):
                dve.wait_ge(s_xs[p], value)
                for j in range(4):
                    V.bn_stats(gst[:, bass.ds(T * 4 + j, 1), :].rearrange("p a s -> p (a s)"), xs[:, p, j]).then_inc(s_gs, 1)

            def first_stats(T, i, p, first, last):
                x_stats(0, T, i, p, at(0, i))
            steps(dve, first_stats)

            def batch(b, nxt):
                f0 = b * (GCH + ACH)
                m0 = b * SM
                dve.wait_ge(s_gs, 4 * NT * (b + 1))
                dve.wait_ge(s_cv, b * CV)
                V.memset(gb[:, 7], 0.0).then_inc(s_g7, 1)
                V.bn_aggr(mv[:], gst[:].rearrange("p k s -> p (k s)")).then_inc(s_f, 1)
                dve.wait_ge(s_m, m0 + 1)
                V.tensor_copy(mg[:], ps[:, 4, 0:1]).then_inc(s_f, 1)
                dve.wait_ge(s_f, f0 + 2)
                V.tensor_tensor(dev[:], mv[:, 0:1], mg[:], ALU.subtract).then_inc(s_f, 1)
                dve.wait_ge(s_f, f0 + 3)
                V.tensor_tensor(dv2[:], dev[:], dev[:], ALU.mult).then_inc(s_f, 1)
                dve.wait_ge(s_f, f0 + 4)
                V.tensor_tensor(dv2[:], dv2[:], mv[:, 1:2], ALU.add).then_inc(s_f, 1)
                dve.wait_ge(s_m, m0 + 2)
                V.tensor_scalar(vs[:], ps[:, 4, 1:2], GN_EPS, None, ALU.add).then_inc(s_f, 1)
                inverse_root(b, vs, sq, rs, nt)
                V.tensor_scalar(ws[:].rearrange("p g m -> p (g m)"), wqkv[:].rearrange("p g m -> p (g m)"),
                                rs[:, 0:1], None, ALU.mult).then_inc(s_ws, 1)
                dve.wait_ge(s_m, m0 + 3)
                V.tensor_tensor(bs[:], bqkv[:], ps[:, 4, 2:6], ALU.subtract).then_inc(s_bs, 1)


                def relu(T, J):
                    dve.wait_ge(s_cv, b * CV + 2 * T + J + 1)
                    dve.wait_ge(s_z1, b * NZB + 2 * T + J)
                    for q in range(2):
                        V.tensor_scalar(rb[:, q], ps[:, 2 + q, :], bc3[:, 0:1], 0.0, ALU.add, ALU.max).then_inc(s_r, 1)

                def low(T, p, j):
                    dve.wait_ge(s_gh, b * K + 4 * T + j + 1)
                    V.scalar_tensor_tensor(gb[:, (4 * p + j) % 8, 1, 1:W + 1], gf[:, j % 4], S_DATA,
                                           gb[:, (4 * p + j) % 8, 0, 1:W + 1], ALU.mult, ALU.subtract).then_inc(s_gl, 1)

                def low_z(t, slot, top=0):
                    dve.wait_ge(s_zh, b * NZB + t + 1)
                    V.scalar_tensor_tensor(zb[:, slot, 1, 1:W + 1], ps[:, 4, :], bc1[:, top:top + 1],
                                           zb[:, slot, 0, 1:W + 1], ALU.add, ALU.subtract).then_inc(s_z, 1)

                def main(T, i, p, first, last):
                    n = b * NT + T
                    if first:
                        low(T, p, 0)
                        low(T, p, 1)
                    low(T, p, 2)
                    low(T, p, 3)
                    if not first:
                        low_z(2 * T - 1, (2 * p - 1) % 4)
                    dve.wait_ge(s_qa, 3 * n + 1)
                    dve.wait_ge(s_tp, n)
                    V.tensor_tensor(qh[:], qb[:, 0:W:2], qb[:, 1:W:2], ALU.add).then_inc(s_h, 1)
                    dve.wait_ge(s_h, 3 * n + 1)
                    V.tensor_tensor(hq[:, p], qh[:], qb[:, 2:W + 2:2], ALU.add).then_inc(s_h, 1)
                    dve.wait_ge(s_qa, 3 * n + 2)
                    V.tensor_tensor(hk[:], kb[:, 0:W:2], kb[:, 1:W:2], ALU.max).then_inc(s_h, 1)
                    relu(T, 0)
                    if first:
                        dve.wait_ge(s_r, b * NRL + 1)
                        V.memset(rb[0:32, 0], 0.0).then_inc(s_top, 1)
                    dve.wait_ge(s_vh, n + 1)
                    V.scalar_tensor_tensor(vh[:, p, 1], vb[:, p], S_DATA, vh[:, p, 0], ALU.mult,
                                           ALU.subtract).then_inc(s_vl, 1)
                    low_z(2 * T, (2 * p) % 4, 1 if first else 0)
                    if not last:
                        low(T, p, 4)
                        low(T, p, 5)
                    if nxt:
                        x_stats(b + 1, T, i, p, at(b + 1, i))
                    dve.wait_ge(s_tp, n + 1)
                    dve.wait_ge(s_sc, n)
                    V.tensor_scalar(qT[:].rearrange("p h m -> p (h m)"), ps[:, 6, 0:128], 1.0 / 9.0, None,
                                    ALU.mult).then_inc(s_te, 1)
                    V.tensor_reduce(kT[:].rearrange("p h (r c) -> p (h r) c", c=8),
                                    ps[:, 6, 128:384].rearrange("p (h r a c) -> p (h r) c a", h=2, a=2, c=8), AX_X,
                                    ALU.max).then_inc(s_te, 1)
                    relu(T, 1)
                    if not first:
                        d_stats(2 * T - 2)
                    if last:
                        low_z(2 * NT - 1, (2 * NT - 1) % 4)
                        dve.wait_ge(s_cv, b * CV + 2 * NT + 1)
                        dve.wait_ge(s_z1, b * NZB + 2 * NT)
                        V.tensor_scalar(rb[0:32, 0], ps[0:32, 2, :], bc3[0:32, 0:1], 0.0, ALU.add, ALU.max).then_inc(s_r, 1)
                        dve.wait_ge(s_d, b * NZ + 2 * NT - 2)
                        V.memset(zb[:, 0], 0.0).then_inc(s_zz, 1)
                        dve.wait_ge(s_zz, b + 1)
                        dve.wait_ge(s_zh, b * NZB + 2 * NT + 1)
                        V.scalar_tensor_tensor(zb[0:16, 0, 1, 1:W + 1], ps[0:16, 4, :], bc1[0:16, 0:1],
                                               zb[0:16, 0, 0, 1:W + 1], ALU.add, ALU.subtract).then_inc(s_z, 1)
                        d_stats(2 * NT - 2)

                def d_stats(t):
                    for q in range(2):
                        dve.wait_ge(s_de, b * NZ + t + q + 1)
                        V.bn_stats(dst2[:, bass.ds(b * NZ + t + q, 1), :].rearrange("p a s -> p (a s)"),
                                   db[:, q]).then_inc(s_dn, 1)

                steps(dve, main)

                g0 = f0 + GCH
                dve.wait_ge(s_sc, (b + 1) * NT)
                V.tensor_tensor(scm[:], ps[0:64, 7, 0:64], smask[:], ALU.mult).then_inc(s_f, 1)
                dve.wait_ge(s_m, m0 + 4)
                V.tensor_reduce(sc8[:], ps[0:8, 4, 0:64].rearrange("k (r q) -> k q r", q=8), AX_X, ALU.add).then_inc(s_f, 1)
                dve.wait_ge(s_f, g0 + 2)
                V.tensor_reduce(smx[:], sc8[:], AX_X, ALU.max).then_inc(s_f, 1)
                dve.wait_ge(s_f, g0 + 3)
                V.tensor_scalar(scd[:], sc8[:], smx[:, 0:1], None, ALU.subtract).then_inc(s_f, 1)
                dve.wait_ge(s_ex, b + 1)
                V.tensor_reduce(ssum[:], sce[:], AX_X, ALU.add).then_inc(s_f, 1)
                dve.wait_ge(s_f, g0 + 5)
                V.reciprocal(sinv[:], ssum[:]).then_inc(s_f, 1)
                dve.wait_ge(s_f, g0 + 6)
                V.tensor_scalar(sce[:], sce[:], sinv[:, 0:1], None, ALU.mult).then_inc(s_f, 1)
                dve.wait_ge(s_f, g0 + 7)
                V.tensor_copy(attn[:], bass_broadcast_rows(sce)).then_inc(s_f, 1)
                dve.wait_ge(s_m, m0 + 5)
                V.tensor_copy(mfac[:, bass.ds(b, 1), 0:16].rearrange("p a m -> p (a m)"), ps[:, 4, 64:80]).then_inc(s_f, 1)
                dve.wait_ge(s_m, m0 + 6)
                V.tensor_copy(mo[:], ps[0:16, 3, 0:128]).then_inc(s_f, 1)
                dve.wait_ge(s_m, m0 + 7)
                V.tensor_copy(mfac[:, bass.ds(b, 1), 16:48].rearrange("p a m -> p (a m)"), ps[:, 4, 96:128]).then_inc(s_f, 1)
                dve.wait_ge(s_f, g0 + 9)
                dw1_weights(b, b).then_inc(s_dw, 1)

                def dw1(T, i, p, first, last):
                    n = b * NT + T
                    for h in range(2):
                        dve.wait_ge(s_a1, 2 * n + h + 1)
                        v = 1 if first and h == 0 else 2 if last and h == 1 else 0
                        fix_columns(2 * p + h, v).then_inc(s_a1c, 1)
                    for h in range(2):
                        dve.wait_ge(s_a1e, 2 * n + h + 1)
                        V.bn_stats(dst1[:, bass.ds(b * NZ + T * 2 + h, 1), :].rearrange("p a s -> p (a s)"),
                                   yb[:, p, h, 0]).then_inc(s_a1n, 1)
                steps(dve, dw1)

            def bass_broadcast_rows(t):
                return t[:].unsqueeze(1).broadcast_to([8, 16, 8])

            def dw1_weights(b, call):
                m = mfac[:, bass.ds(b, 1), 0:16]
                V.tensor_tensor(d1w[:].rearrange("p a r i -> p (a r) i"), td1[:].rearrange("p a r i -> p (a r) i"),
                                m.broadcast_to([128, 48, 16]), ALU.mult).then_inc(s_wsp, 1)
                dve.wait_ge(s_wsp, 2 * call + 1)
                taps = d1w[:].rearrange("p a r i -> p a (r i)")
                V.tensor_scalar(d1wh[:, 0], taps, S_ATT, None, ALU.mult).then_inc(s_wsp, 1)
                dve.wait_ge(s_wsp, 2 * call + 2)
                return V.scalar_tensor_tensor(d1wh[:, 1], taps, S_ATT, d1wh[:, 0], ALU.mult, ALU.subtract)

            def fix_columns(bank, v):
                edge = ps[:, bank, 0:W:W - 1]
                return V.tensor_tensor(edge, edge, d1x[:, v, :], ALU.add)

            batches(dve, batch)

            fb = B * (GCH + ACH)
            dve.wait_ge(s_a1n, 2 * NT * B)
            dve.wait_ge(s_dn, NZ * B)
            for q, st in enumerate((dst1, dst2)):
                V.bn_aggr(mvb[:, q, :], st[:].rearrange("p k s -> p (k s)")).then_inc(s_f, 1)
            dve.wait_ge(s_m, B * SM + 2)
            V.tensor_copy(mgb[:], ps[:, 7, 4:6]).then_inc(s_f, 1)
            dve.wait_ge(s_f, fb + 3)
            V.tensor_tensor(devb[:], mvb[:, :, 0], mgb[:], ALU.subtract).then_inc(s_f, 1)
            dve.wait_ge(s_f, fb + 4)
            V.tensor_tensor(dvb2[:], devb[:], devb[:], ALU.mult).then_inc(s_f, 1)
            dve.wait_ge(s_f, fb + 5)
            V.tensor_tensor(dvb2[:], dvb2[:], mvb[:, :, 1], ALU.add).then_inc(s_f, 1)
            dve.wait_ge(s_m, B * SM + 3)
            V.tensor_scalar(vsb[:], ps[:, 7, 6:8], BN_EPS, None, ALU.add).then_inc(s_f, 1)
            inverse_root(B, vsb, sqb, rsb, ntb)
            V.tensor_tensor(ab[:, :, 0], rsb[:], bndw[:, :, 0], ALU.mult).then_inc(s_f, 1)
            dve.wait_ge(s_f, fb + 8)
            V.tensor_tensor(tmpb[:], mgb[:], ab[:, :, 0], ALU.mult).then_inc(s_f, 1)
            dve.wait_ge(s_f, fb + 9)
            V.tensor_tensor(ab[:, :, 1], bndw[:, :, 1], tmpb[:], ALU.subtract).then_inc(s_f, 1)
            V.tensor_tensor(x1c[:], b3r[:], ps[:, 7, 0:2], ALU.add).then_inc(s_f, 1)
            dve.wait_ge(s_f, fb + 10)
            V.tensor_scalar(ad1[:], ab[:, 0, 0:1], 1 / (S_DATA * S_ATT), None, ALU.mult).then_inc(s_f, 1)
            dve.wait_ge(s_f, fb + 12)
            V.tensor_scalar(bt[:], d1c[:], ab[:, 0, 0:1], ab[:, 0, 1:2], ALU.mult, ALU.add).then_inc(s_bn, 1)

            def last_batch(b):
                if not static(b):
                    dve.wait_ge(s_fx, b * NT * 4)
                dw1_weights(b, B + b).then_inc(s_x1p, 1)
                for e in range(2):
                    m3 = mfac[:, bass.ds(b, 1), 16 + e:48:2]
                    V.tensor_tensor(x1w[:, e].rearrange("p m r i -> p (m r) i"),
                                    rmask[:].rearrange("p m r -> p (m r)").unsqueeze(2).broadcast_to([128, 16, 16]),
                                    m3.broadcast_to([128, 16, 16]), ALU.mult).then_inc(s_x1p, 1)
                dve.wait_ge(s_x1p, 4 * b + 3)
                products = x1w[:].rearrange("p e m r i -> p e m (r i)")
                V.tensor_scalar(x1wh[:, 0], products, S_ATT, None, ALU.mult).then_inc(s_x1p, 1)
                dve.wait_ge(s_x1p, 4 * b + 4)
                V.scalar_tensor_tensor(x1wh[:, 1], products, S_ATT, x1wh[:, 0], ALU.mult, ALU.subtract).then_inc(s_fw, 1)

                def last_pass(T, i, r, first, last):
                    n = b * NT + T
                    p = r % 2
                    for h in range(2):
                        dve.wait_ge(s_fa, 2 * n + h + 1)
                        v = 1 if first and h == 0 else 2 if last and h == 1 else 0
                        fix_columns(2 * p + h, v).then_inc(s_fc, 1)
                        if h == 0:
                            dve.wait_ge(s_lx[r], 16 * (b * NF + i) + 16)
                        dve.wait_ge(s_fx, 4 * n + 2 * h + 2)
                        for e in range(2):
                            xt = xl[:, r, 2 * h + e]
                            op = V.scalar_tensor_tensor(xt, ps[:, 4 + 2 * h + e, :], 1 / (S_DATA * S_ATT), xt, ALU.mult,
                                                        ALU.add)
                        op.then_inc(s_ft, 1)
                    for h in range(2):
                        dve.wait_ge(s_ft, 2 * n + h + 1)
                        dve.wait_ge(s_fg, 4 * n + 2 * h + 2)
                        for e in range(2):
                            xt = xl[:, r, 2 * h + e]
                            op = V.scalar_tensor_tensor(xt, xt, x1c[:, e:e + 1], yb[:, p, h, e], ALU.add, ALU.add)
                        op.then_inc(s_fo, 1)
                steps4(dve, last_pass)
            last_batch(0)
            with dve.Fori(1, B) as b:
                last_batch(b)


def _toeplitz(rows_in, rows_out, shift, taps, dx):
    import numpy as np
    co, ci = taps.shape[:2]
    m = np.zeros((rows_in, ci, rows_out, co), taps.dtype)
    for a in range(rows_in):
        for o in range(rows_out):
            if 0 <= a - o + shift <= 2:
                m[a, :, o, :] = taps[:, :, a - o + shift, dx].T
    return m


def layouts(inp):
    import numpy as np
    g = {k: np.asarray(v) for k, v in inp.items()}
    L = lambda n: g["L0_conv_" + n]
    f = np.float32
    z = lambda *s: np.zeros(s, f)
    out = {"x": np.ascontiguousarray(g["x"].transpose(0, 2, 1, 3))}
    w = L("qkvl_w")[:, :, 0, 0]
    q = z(4, 32, 4, 128)
    for r in range(4):
        q[r, 16:32, 0, 32 * r:32 * r + 32] = w.T
        for h in range(3):
            for j in range(4):
                q[r, 0:16, 1 + h, 32 * j + 8 * r:32 * j + 8 * r + 8] = w[8 * h:8 * h + 8].T
    out["w_qkv"] = q.reshape(128, 4, 128)
    b = L("qkvl_b")
    out["b_qkv"] = np.stack([np.tile(b, 4)] + [np.tile(b[8 * h:8 * h + 8], 16) for h in range(3)], 1)
    c3 = L("conv3x3_w")
    out["w_c3"] = np.stack([_toeplitz(4, 2, s, c3, d).reshape(128, 64) for s in (0, -2) for d in range(3)], 1)
    out["b_c3"] = np.stack([np.tile(L("conv3x3_b"), 4)] * 2, 1)
    c1 = L("conv1x1_w")[:, :, 0, 0]
    m = z(2, 4, 32, 4, 16)
    for v, order in enumerate(((0, 1, 2, 3), (2, 3, 0, 1))):
        for pos, l in enumerate(order):
            m[v, pos, :, l, :] = c1.T
    out["w_c1"] = np.ascontiguousarray(m.reshape(2, 128, 64).transpose(1, 0, 2))
    bz = np.tile(L("conv1x1_b"), 8)
    top = bz.copy()
    top[:16] = 0
    out["b_c1"] = np.stack([bz, top], 1)
    dw, dwb = L("dwc3x3_w"), L("dwc3x3_b")
    bn = np.stack([L("bn_gamma"), L("bn_beta")], 1)
    out["bn_dw"] = np.stack([np.tile(bn[e::2], (8, 1)) for e in range(2)], 1)
    diag = z(16, 16, 3, 3)
    for i in range(16):
        diag[i, i] = dw[2 * i + 1, 0]
    out["w_dw2"] = np.stack([_toeplitz(8, 4, s, diag, d).reshape(128, 64) for s in (0,) for d in range(3)], 1)
    full = np.broadcast_to(dw[0::2], (16, 8, 3, 3))
    out["w_dw1"] = np.stack([_toeplitz(16, 2, -2 * m if h == 0 else -6 - 2 * m, full, d).reshape(128, 2, 16)
                             for h in range(2) for m in range(4) for d in range(3)], 1)
    s = np.broadcast_to(dw[0::2, 0].transpose(0, 2, 1)[None, :, None], (8, 16, 3, 3, 3)).copy()
    s[0, :, 1, :, 0] = 0
    s[7, :, 2, :, 2] = 0
    out["dw_sum"] = s.reshape(128, 3, 3, 3)
    b2 = L("conv1x1_2_b")
    out["b_2rep"] = np.tile(b2, 8).reshape(128, 1)
    out["b_dw"] = np.stack([np.tile(dwb[0::2], 8), np.tile(dwb[1::2], 8)], 1)
    out["w2t"] = np.ascontiguousarray(L("conv1x1_2_w")[:, :, 0, 0].T)
    w3 = L("conv1x1_3_w")[:, :, 0, 0]
    out["w3t"] = np.ascontiguousarray(w3.T)
    out["w3rep"] = np.stack([np.tile(w3[e::2].T, (1, 8)) for e in range(2)], 1)
    b3 = L("conv1x1_3_b")
    out["b3rep"] = np.stack([np.tile(b3[e::2], 8) for e in range(2)], 1)
    rm = z(16, 8, 8, 2)
    for h in range(2):
        for mq in range(4):
            for r in range(2):
                l = 2 * mq + r + 1 if h == 0 else 7 + 2 * mq + r
                rm[l, :, 4 * h + mq, r] = 1
    out["row_mask"] = rm.reshape(128, 8, 2)
    p = np.arange(128)
    out["gn_mix"] = ((p[:, None] % 32 // 2 == p[None] % 32 // 2) / 8).astype(f)
    out["bn_mix"] = ((p[:, None] % 16 == p[None] % 16) / 8).astype(f)
    out["ident"] = np.eye(128, dtype=f)
    ps = z(16, 8, 2, 8, 8)
    for c in range(8):
        for r in range(8):
            for a in (2 * r - 1, 2 * r, 2 * r + 1):
                if a >= 0:
                    ps[a, c, 0, r, c] = 1
        ps[15, c, 1, 0, c] = 1
    out["pool_sum"] = ps.reshape(128, 2, 64)
    a = np.arange(64)
    out["score_mask"] = (a[:, None] // 8 == a[None] // 8).astype(f)
    out["score_fold"] = (a[:, None] % 8 == np.arange(128)[None]).astype(f)
    return {k: np.ascontiguousarray(v, dtype=f) for k, v in out.items()}


def scratch(nc, B, H):
    return {"v_dram": nc.dram_tensor("v_dram", (B, H + 2, 8, 2, W), F16, kind="Internal").ap(),
            "d_dram": nc.dram_tensor("d_dram", (B, H, 16, W), F32, kind="Internal").ap()}


def kernel(**inputs):
    import concourse.bacc as _bacc
    from concourse.bass_utils import run_bass_kernel_spmd as _run
    import numpy as np

    nc = _bacc.Bacc("TRN2", target_bir_lowering=False, num_devices=1)
    arrays = {f"in_{k}": v for k, v in layouts(inputs).items()}
    args = {k[3:]: nc.dram_tensor(k, v.shape, F32, kind="ExternalInput").ap() for k, v in arrays.items()}
    B, H = arrays["in_x"].shape[:2]
    out = nc.dram_tensor("out_0", (B, H, C, W), F32, kind="ExternalOutput").ap()
    preact_kernel(nc, out=out, **scratch(nc, B, H), **args)
    r = _run(nc, [arrays], core_ids=[0])
    return np.ascontiguousarray(r.results[0]["out_0"].transpose(0, 2, 1, 3))
```
